# Optimizing a Trainium2 kernel written in Bass

```python
import numpy as np
import jax
import jax.numpy as jnp

def _softmax(x, axis=-1):
    return jax.nn.softmax(x, axis=axis)

def _gelu(x):
    return jax.nn.gelu(x, approximate=True)

def _silu(x):
    return jax.nn.silu(x)

def _sigmoid(x):
    return jax.nn.sigmoid(x)

def _layernorm(x, axis=-1, eps=1e-05):
    m = jnp.mean(x, axis=axis, keepdims=True)
    v = jnp.var(x, axis=axis, keepdims=True)
    return (x - m) / jnp.sqrt(v + eps)

def _scatter_add(tgt, idx, src, axis=0):
    return tgt.at[idx].add(src)

def _segment_sum(src, seg, n):
    return jax.ops.segment_sum(src, seg, n)
kernel_name = 'mk_seq_postln_d1_jaxref_r8_1f2560'

def setup_inputs(seed: int=0):
    np.random.seed(seed)
    _w = jnp.asarray

    def _L0_attn_setup():
        import jax, jax.numpy as jnp
        import numpy as np
        import math
        NUM_HEADS = 16
        key = jax.random.key(seed)
        ks = jax.random.split(key, 5)
        B, S, D = (2, 256, 256)
        scale = 1.0 / math.sqrt(D)
        return {'x': jax.random.normal(ks[0], (B, S, D), dtype=jnp.float32), 'Wq': jax.random.normal(ks[1], (D, D), dtype=jnp.float32) * scale, 'Wk': jax.random.normal(ks[2], (D, D), dtype=jnp.float32) * scale, 'Wv': jax.random.normal(ks[3], (D, D), dtype=jnp.float32) * scale, 'Wp': jax.random.normal(ks[4], (D, D), dtype=jnp.float32) * scale}
    _L0_attn_in = _L0_attn_setup()

    def _L0_ffn_setup():
        import jax, jax.numpy as jnp
        import numpy as np
        H, I, E, K = (256, 96, 8, 2)
        NUM_LOADED = 8
        key = jax.random.key(seed)
        ks = jax.random.split(key, 5)
        scale = 0.02
        return {'hidden_states': jax.random.normal(ks[0], (2, 128, H), dtype=jnp.float32), 'router_w': jax.random.normal(ks[1], (E, H), dtype=jnp.float32) * scale, 'gate_w': jax.random.normal(ks[2], (E, I, H), dtype=jnp.float32) * scale, 'up_w': jax.random.normal(ks[3], (E, I, H), dtype=jnp.float32) * scale, 'down_w': jax.random.normal(ks[4], (E, H, I), dtype=jnp.float32) * scale}
    _L0_ffn_in = _L0_ffn_setup()
    _d = {'L0_attn_x': _L0_attn_in['x'], 'L0_attn_Wq': _L0_attn_in['Wq'], 'L0_attn_Wk': _L0_attn_in['Wk'], 'L0_attn_Wv': _L0_attn_in['Wv'], 'L0_attn_Wp': _L0_attn_in['Wp'], 'L0_ffn_router_w': _L0_ffn_in['router_w'], 'L0_ffn_gate_w': _L0_ffn_in['gate_w'], 'L0_ffn_up_w': _L0_ffn_in['up_w'], 'L0_ffn_down_w': _L0_ffn_in['down_w']}
    _x0 = _d['L0_attn_x']
    _d['L0_attn_x'] = jax.random.normal(jax.random.fold_in(jax.random.key(seed), 1), (2, 512, 256), dtype=_x0.dtype)
    del _x0
    return _d

def reference(L0_attn_x, L0_attn_Wq, L0_attn_Wk, L0_attn_Wv, L0_attn_Wp, L0_ffn_router_w, L0_ffn_gate_w, L0_ffn_up_w, L0_ffn_down_w):

    def _L0_attn_ref(x, Wq, Wk, Wv, Wp):
        import jax, jax.numpy as jnp
        import numpy as np
        import math
        NUM_HEADS = 16
        B, S, D = x.shape
        H = NUM_HEADS
        hd = D // H
        q = (x @ Wq.T).reshape(B, S, H, hd).transpose(0, 2, 1, 3)
        k = (x @ Wk.T).reshape(B, S, H, hd).transpose(0, 2, 1, 3)
        v = (x @ Wv.T).reshape(B, S, H, hd).transpose(0, 2, 1, 3)
        scores = jnp.einsum('bhqd,bhkd->bhqk', q, k) / jnp.sqrt(jnp.asarray(hd, x.dtype))
        causal = jnp.triu(jnp.ones((S, S), dtype=bool), k=1)
        scores = jnp.where(causal, -jnp.inf, scores)
        attn = jax.nn.softmax(scores, axis=-1)
        out = jnp.einsum('bhqk,bhkd->bhqd', attn, v)
        out = out.transpose(0, 2, 1, 3).reshape(B, S, D)
        return out @ Wp.T

    def _L0_ffn_ref(hidden_states, router_w, gate_w, up_w, down_w):
        import jax, jax.numpy as jnp
        import numpy as np
        H, I, E, K = (256, 96, 8, 2)
        NUM_LOADED = 8
        B, S, Hd = hidden_states.shape
        x = hidden_states.reshape(-1, Hd)
        logits = x @ router_w.T
        probs = jax.nn.softmax(logits.astype(jnp.float32), axis=-1)
        w, sel = jax.lax.top_k(probs, K)
        w = w * (sel < NUM_LOADED).astype(w.dtype)
        s = jnp.sum(w, axis=-1, keepdims=True)
        w = (w / jnp.where(s == 0, 1.0, s)).astype(x.dtype)
        coeff = jnp.sum(jax.nn.one_hot(sel, E, dtype=x.dtype) * w[..., None], axis=1)
        g = jnp.einsum('th,eih->eti', x, gate_w)
        u = jnp.einsum('th,eih->eti', x, up_w)
        h = jax.nn.silu(g) * u
        y = jnp.einsum('eti,ehi->eth', h, down_w)
        out = jnp.einsum('eth,te->th', y, coeff)
        return out.reshape(B, S, Hd)
    x = L0_attn_x
    x = _layernorm(x + _L0_attn_ref(x, L0_attn_Wq, L0_attn_Wk, L0_attn_Wv, L0_attn_Wp), axis=-1)
    x = _layernorm(x + _L0_ffn_ref(x, L0_ffn_router_w, L0_ffn_gate_w, L0_ffn_up_w, L0_ffn_down_w), axis=-1)
    return x

_drawn_inputs = setup_inputs


def setup_inputs(seed=0):
    import zlib

    import numpy as np

    out = dict(_drawn_inputs(seed))
    spreads = {}
    factors = {'L0_ffn_router_w': 8.0,
     'L0_ffn_gate_w': 7.777,
     'L0_ffn_up_w': 7.713,
     'L0_ffn_down_w': 7.692}
    for name, (base, spread) in spreads.items():
        noise = np.random.default_rng([zlib.crc32(name.encode()), seed]).standard_normal(out[name].shape)
        drawn = base * np.exp(spread * noise) if base else spread * noise
        out[name] = jnp.asarray(drawn.astype(out[name].dtype))
    for name, factor in factors.items():
        out[name] = (out[name] * factor).astype(out[name].dtype)
    return out
```

```python
from contextlib import ExitStack

import concourse.bass as bass
from concourse import mybir

F32 = mybir.dt.float32
F32R = mybir.dt.float32r
BF16 = mybir.dt.bfloat16
U32 = mybir.dt.uint32
ALU = mybir.AluOpType
ACT = mybir.ActivationFunctionType
AX = mybir.AxisListType

P = 128
B, S, D = 2, 512, 256
H, HD = 16, 16
KC = D // P
NT = S // P
QH = 4
NQ = H // QH
G = B * NQ
E, I = 8, 96
EI = E * I
FC = EI // P
EPS = 1e-5
SCALE = HD ** -0.5
MASKED = -1e30

STACK = 4 * HD
MAXROW = 96
SLOTS = 3
SEG = [0, 512, 896, 1152]
PTW = 1280
VW = 32

UNITS1 = [(3, [h]) for h in range(4)] + [(2, [h]) for h in range(4)] + [(1, [0, 1]), (1, [2, 3]), (0, [0, 1, 2, 3])]
UNITS2 = [(3 - t, hs) for t, hs in UNITS1]
NU = len(UNITS1)
CONSTS = 7 + 2 * SLOTS
CONSTS_ALL = CONSTS + E + 7
MASK_AFTER = [4, 8, 10, 11]


LEAD = NU + 5


def chain(b):
    return [("OTR", b, 0), ("OTR", b, 1), ("Y", b, 0), ("Y", b, 1), ("LN1", b, 0), ("XT", b, 0), ("XT", b, 1),
            ("RL", b, 0), ("RT", b, 0), ("RC", b, 0)]


def make_plan():
    plan = [("PROJ", 0, n) for n in range(4)] + [("V", 0, n) for n in range(4)]
    second = [("PROJ", 1, n) for n in range(4)] + [("V", 1, n) for n in range(4)]
    links = []
    for s in range(G * NU + LEAD):
        if s < G * NU:
            plan.append(("S1", s // NU, s % NU))
        if s >= 2 and second:
            plan.append(second.pop(0))
        if s >= NU and s % NU == 0 and s <= G * NU:
            plan.append(("NM", s // NU - 1, 0))
        if s >= LEAD:
            g, u = divmod(s - LEAD, NU)
            plan.append(("S2", g, u))
            if g >= 1 and u in (2, 4, 6, 8):
                plan.append(("PV", g - 1, u // 2 - 1))
            if g >= 1 and u == 9:
                plan.append(("OC", g - 1, 0))
            if g >= 1 and u == 10:
                plan.append(("OT", g - 1, 0))
                if g == NQ:
                    links = chain(0)
            if links and u % 2 and u < 10:
                plan.append(links.pop(0))
            if g in (1, 2, 3) and u in (1, 3, 5, 7):
                plan.append(("GH", 0, 4 * (g - 1) + u // 2))
    plan += links
    links = chain(1)
    plan += [("GU", 0, 0)] + [("PV", G - 1, j) for j in range(NT)] + [("OC", G - 1, 0), ("GU", 0, 1), ("OT", G - 1, 0)]
    n_links = {2: (1, 1), 3: (1, 1), 4: (1, 0), 5: (1, 1), 6: (1, 1), 7: (1, 0)}
    for n in range(2, B * FC + 2):
        back = ((n - 2) // FC, (n - 2) % FC)
        plan += [("CB", *back), ("HL", *back)]
        if n < B * FC:
            plan.append(("GU", n // FC, n % FC))
        before, after = n_links.get(n, (0, 0))
        plan += [links.pop(0) for _ in range(before)]
        plan.append(("DN", *back))
        plan += [links.pop(0) for _ in range(after)]
        if back[1] == FC - 1:
            plan.append(("LN2", back[0], 0))
    assert not links
    return plan


PLAN = make_plan()
MISC = {s: n for n, s in enumerate([s for s in PLAN if s[0] in ("OT", "OTR", "Y", "XT", "RL", "RT", "RC")])}
PROJ_BANK = {s: n for n, s in enumerate([s for s in PLAN if s[0] in ("PROJ", "V")])}


def layer_kernel(nc, xT_d, x_d, wqkv_d, wp_d, wr_d, wgu_d, wd_d, out_d):
    with ExitStack() as ctx:
        def sb(name, shape, dt=F32):
            return ctx.enter_context(nc.sbuf_tensor(name, shape, dt))

        def sem(name):
            return ctx.enter_context(nc.semaphore(name))

        early = sb("early", [P, 14 * 256])
        xT = early[:, 0:KC * B * S].rearrange("p (k n) -> p k n", k=KC)
        wqkv = early[:, KC * B * S:].rearrange("p (w k n) -> p w k n", w=3, k=KC)
        gu_raw = early[:, 0:KC * 2 * EI].rearrange("p (k n) -> p k n", k=KC)
        wp = sb("wp", [P, KC, D])
        wd_raw = sb("wd_raw", [P, FC, D])
        wr_raw = sb("wr_raw", [P, KC, E])
        wr = sb("wr", [P, KC, 2 * E], F32R)
        x = sb("x", [P, B * NT, D])
        qk = [sb(f"qk{b}", [P, 4, KC, S], F32R) for b in range(B)]
        gu_hi = qk[0][:, 0:3].rearrange("p a k n -> p (a k n)").rearrange("p (k n) -> p k n", k=KC)
        gu_lo = qk[1][:, 0:3].rearrange("p a k n -> p (a k n)").rearrange("p (k n) -> p k n", k=KC)
        vv = sb("vv", [P, B * NT, H, VW])
        stacks = sb("stacks", [P, SLOTS, 2, QH, S], F32R)
        flat = [stacks[:, n].rearrange("p a h n -> p (a h n)") for n in range(SLOTS)]
        h_hl = flat[0][:, 0:3 * 2 * S].rearrange("p (r a n) -> p r a n", r=3, a=2)
        wd_hl = flat[2][:, 0:2 * FC * D].rearrange("p (a c n) -> p a c n", a=2, c=FC)
        pt = sb("pt", [P, 2, QH, PTW])
        temps = pt[:, 0].rearrange("p h n -> p (h n)")
        silu_g = temps[:, 0:2 * S].rearrange("p (r n) -> p r n", r=2)
        gated = temps[:, 2 * S:5 * S].rearrange("p (r n) -> p r n", r=3)
        hidden = temps[:, 5 * S:7 * S].rearrange("p (r n) -> p r n", r=2)
        ot = sb("ot", [P, 2, S])
        attn = sb("attn", [P, NT, D])
        attnT = sb("attnT", [P, KC, S])
        x1T = sb("x1T", [P, 2, B, KC, S], F32R)
        mx = sb("mx", [P, 2, QH, NT])
        nm = [sb("nm_hi", [QH * NT, P], F32R), sb("nm_lo", [QH * NT, P], F32R)]
        rden = sb("rden", [P, 2, NT, QH])
        stats = sb("stats", [P, 2 * B * NT, 6])
        mv = sb("mv", [P, 2 * B * NT, 2])
        var_eps = sb("var_eps", [P, 2 * B * NT])
        rstd = sb("rstd", [P, 2 * B * NT])
        lgT = sb("lgT", [2 * E, S])
        lg2 = sb("lg2", [P, NT, E])
        lg = sb("lg", [P, NT, E])
        top = sb("top", [P, NT, E])
        topi = sb("topi", [P, NT, E], U32)
        topf = sb("topf", [P, NT, 2])
        gap = sb("gap", [P, NT])
        th = sb("th", [P, NT])
        wsel = sb("wsel", [P, NT, 2])
        c1 = sb("c1", [P, NT, E])
        coef = sb("coef", [P, NT, E])
        coefhl = sb("coefhl", [P, NT, 2 * E])
        coefT = qk[0][0:2 * E, 3, :, :]
        ident = sb("ident", [P, P])
        identb = sb("identb", [P, P], BF16)
        maskb = sb("maskb", [P, P], BF16)
        spread = attnT[0:2 * E].rearrange("p k n -> p (k n)")[:, 0:EI]
        spread_r = sb("spread_r", [2 * E, EI], F32R)
        iota_e = sb("iota_e", [P, E])
        minus_half = sb("minus_half", [P, 2])

        bank = [ctx.enter_context(nc.psum_tensor(f"bank{n}", [P, 512], F32)) for n in range(8)]
        s1_bank, s2_bank, pv_bank, nm_bank, misc = bank[0:3], bank[3:5], bank[5], bank[6], bank[7]
        proj_bank = bank[3:7]
        ffn_bank, coef_bank, y_bank = bank[0:3], bank[6], bank[3:5]

        def gate_bank(n):
            return ffn_bank[2 * n % 3]

        def up_bank(n):
            return ffn_bank[(2 * n + 1) % 3]

        ld_xT = [sem(f"ld_xT{b}") for b in range(B)]
        ld_wp, ld_x, ld_wr, ld_gu, ld_wd = (sem(n) for n in ("ld_wp", "ld_x", "ld_wr", "ld_gu", "ld_wd"))
        ld_w = [sem(f"ld_w{n}") for n in "qkv"]
        consts = sem("consts")
        pool_own = sem("pool_own")
        proj = sem("proj")
        qk_hi = sem("qk_hi")
        qk_lo = sem("qk_lo")
        v_done = sem("v_done")
        filled = [sem(f"filled{n}") for n in range(SLOTS)]
        s1 = sem("s1")
        s1_read = sem("s1_read")
        nm_t = sem("nm_t")
        nm_hi = sem("nm_hi_done")
        nm_lo = sem("nm_lo_done")
        nm_in = sem("nm_in")
        s2 = sem("s2")
        exp_done = sem("exp_done")
        masked = sem("masked")
        pv = sem("pv")
        ot_copied = sem("ot_copied")
        m_full = sem("m_full")
        m_read = sem("m_read")
        dve_own = sem("dve_own")
        attn_done = sem("attn_done")
        attnT_done = sem("attnT_done")
        stat_done = sem("stat_done")
        rstd_done = sem("rstd_done")
        ln_done = sem("ln_done")
        x1T_hi = sem("x1T_hi")
        x1T_done = sem("x1T_done")
        lgT_done = sem("lgT_done")
        gap_done = sem("gap_done")
        th_done = sem("th_done")
        coef_done = sem("coef_done")
        coefT_done = sem("coefT_done")
        gu_hi_done = sem("gu_hi_done")
        gu_split = sem("gu_split")
        wd_split = sem("wd_split")
        gate = sem("gate")
        up = sem("up")
        coefs = sem("coefs")
        silu_done = sem("silu_done")
        gated_done = sem("gated_done")
        hid = sem("hid")
        hid_hi = sem("hid_hi")
        hid_lo = sem("hid_lo")
        down = sem("down")
        y_read = sem("y_read")
        stored = sem("stored")

        block = ctx.enter_context(nc.Block())

        @block.sync
        def _(sp):
            sp.dma_start(xT[:, :, 0:S], xT_d[:, :, 0:S]).then_inc(ld_xT[0], 16)
            sp.dma_start(wqkv[:, 0], wqkv_d[:, 0]).then_inc(ld_w[0], 16)
            sp.dma_start(wqkv[:, 2], wqkv_d[:, 2]).then_inc(ld_w[2], 16)

            def fill(g):
                b, c, r = g // NQ, g % NQ // 2, 64 * (g % 2)
                sp.wait_ge(qk_lo, 4 * b + 2 * c + 2)
                sp.wait_ge(qk_hi, 4 * b + 2 * c + 2)
                if g >= SLOTS:
                    sp.wait_ge(s2, NU * (g - SLOTS + 1))
                for side, parts in ((0, (0, 1, 0, 1)), (1, (2, 2, 3, 3))):
                    for n, part in enumerate(parts):
                        sp.dma_start(stacks[HD * n:HD * n + HD, g % SLOTS, side, :, :].bitcast(F32),
                                     qk[b][r:r + 64, part, c, :].bitcast(F32)).then_inc(filled[g % SLOTS], 16)

            fill(0)
            sp.dma_start(xT[:, :, S:2 * S], xT_d[:, :, S:2 * S]).then_inc(ld_xT[1], 16)
            fill(1)
            fill(2)
            sp.dma_start(x[:, :, :], x_d).then_inc(ld_x, 16)
            sp.dma_start(wp[:, :, :], wp_d).then_inc(ld_wp, 16)
            sp.dma_start(wr_raw[:, :, :], wr_d).then_inc(ld_wr, 16)
            sp.dma_start(wd_raw[:, :, :], wd_d).then_inc(ld_wd, 16)
            for step, g, u in PLAN:
                if step == "NM":
                    sp.wait_ge(nm_hi, g + 1)
                    sp.wait_ge(nm_lo, g + 1)
                    for n in range(2):
                        sp.dma_start(stacks[MAXROW + n:MAXROW + n + 1, g % SLOTS, 1, :, :].bitcast(F32),
                                     nm[n][:, :].bitcast(F32)).then_inc(nm_in, 16)
                    if g == 0:
                        sp.wait_ge(proj, len(PROJ_BANK))
                        sp.dma_start(gu_raw, wgu_d).then_inc(ld_gu, 16)
                if step == "S2" and u == NU - 1 and g + SLOTS < G:
                    fill(g + SLOTS)
                if step == "LN2":
                    for t in range(g * NT, g * NT + NT, 2):
                        sp.wait_ge(ln_done, (B * NT + t) // 2 + 1)
                        sp.dma_start(out_d[:, t:t + 2, :], x[:, t:t + 2, :]).then_inc(stored, 16)
            sp.wait_ge(stored, 16 * B * NT // 2)

        @block.gpsimd
        def _(pool):
            made = 0

            def make(ins):
                nonlocal made
                made += 1
                ins.then_inc(consts, 1)
                pool.wait_ge(consts, made)

            make(nc.gpsimd.memset(ident[:, :], 0.0))
            make(nc.gpsimd.affine_select(out=ident[:, :], in_=ident[:, :], compare_op=ALU.not_equal, fill=1.0, base=0,
                                         pattern=[[-1, P]], channel_multiplier=1))
            make(nc.gpsimd.tensor_copy(identb[:, :], ident[:, :]))
            make(nc.gpsimd.memset(maskb[:, :], 0.0))
            make(nc.gpsimd.affine_select(out=maskb[:, :], in_=maskb[:, :], compare_op=ALU.is_ge, fill=MASKED, base=0,
                                         pattern=[[-1, P]], channel_multiplier=1))
            for n in range(SLOTS):
                make(nc.gpsimd.memset(stacks[STACK:MAXROW, n].bitcast(F32), 0.0))
                make(nc.gpsimd.memset(stacks[MAXROW:MAXROW + 2, n, 0].bitcast(F32), 1.0))
            make(nc.gpsimd.memset(vv[:, :, :, HD:HD + 1], 1.0))
            make(nc.gpsimd.memset(vv[:, :, :, HD + 1:VW], 0.0))
            assert made == CONSTS
            make(nc.gpsimd.memset(minus_half[:, :], -0.5))
            for e in range(E):
                make(nc.gpsimd.memset(iota_e[:, e:e + 1], float(e)))
            make(nc.gpsimd.memset(spread[:, :], 0.0))
            for n in range(2):
                v = spread[:, :].rearrange("p (e i) -> p e i", e=E)
                make(nc.gpsimd.affine_select(out=v, in_=v, compare_op=ALU.not_equal, fill=1.0, base=-E * n,
                                             pattern=[[-1, E], [0, I]], channel_multiplier=1))
            make(nc.gpsimd.tensor_copy(spread_r[:, :], spread[:, :]))
            pool.wait_ge(ld_wr, 16)
            make(nc.gpsimd.tensor_copy(wr[:, :, 0:E], wr_raw[:, :, :]))
            make(nc.gpsimd.tensor_tensor(wr[:, :, E:2 * E], wr_raw[:, :, :], wr[:, :, 0:E].bitcast(F32), ALU.subtract))
            assert made == CONSTS_ALL
            own = 0

            def then(ins):
                nonlocal own
                own += 1
                ins.then_inc(pool_own, 1)
                pool.wait_ge(pool_own, own)


            for step, g, u in PLAN:
                if step == "S2" and u + 1 in MASK_AFTER:
                    j = MASK_AFTER.index(u + 1)
                    pool.wait_ge(exp_done, NU * g + u + 1)
                    v = pt[:, g % 2, :, SEG[j]:SEG[j] + P]
                    nc.gpsimd.affine_select(out=v, in_=v, compare_op=ALU.is_ge, fill=0.0, base=0,
                                            pattern=[[0, QH], [1, P]], channel_multiplier=-1).then_inc(masked, 1)
                    if g == 5 and j == 0:
                        for n in range(SLOTS):
                            pool.wait_ge(filled[n], 128 * ((G - 1 - n) // SLOTS + 1))
                    for n in range(2 * j, 2 * j + 2) if g == 5 else range(8 + j, 9 + j) if g == 6 else ():
                        k, cols = n // 6, slice(n % 6 * 256, n % 6 * 256 + 256)
                        pool.wait_ge(gu_hi_done, n + 1)
                        nc.gpsimd.tensor_tensor(gu_lo[:, k, cols], gu_raw[:, k, cols], gu_hi[:, k, cols].bitcast(F32),
                                                ALU.subtract).then_inc(gu_split, 1)
                    if g == G - 1 and j == NT - 1:
                        pool.wait_ge(ld_wd, 16)
                        for c in range(FC):
                            then(nc.gpsimd.tensor_copy(wd_hl[:, 0, c, :], wd_raw[:, c, :]))
                            nc.gpsimd.tensor_tensor(wd_hl[:, 1, c, :], wd_raw[:, c, :], wd_hl[:, 0, c, :].bitcast(F32),
                                                    ALU.subtract).then_inc(wd_split, 1)
                if step == "LN1" or step == "LN2":
                    first = NT * g if step == "LN1" else NT * (B + g)
                    for n in range(first, first + NT, 2):
                        pool.wait_ge(stat_done, n + 2)
                        then(nc.gpsimd.tensor_scalar(var_eps[:, n:n + 2], mv[:, n:n + 2, 1], EPS, None, ALU.add))
                        nc.gpsimd.tensor_tensor(rstd[:, n:n + 2], var_eps[:, n:n + 2], minus_half[:, :],
                                                ALU.pow).then_inc(rstd_done, 1)

        @block.scalar
        def _(act):
            act.dma_start(wqkv[:, 1], wqkv_d[:, 1]).then_inc(ld_w[1], 16)
            for step, g, u in PLAN:
                if step == "PROJ":
                    act.wait_ge(proj, PROJ_BANK[step, g, u] + 1)
                    nc.scalar.copy(qk[g][:, 2 * (u % 2), u // 2, :], proj_bank[PROJ_BANK[step, g, u] % 4][:, :]).then_inc(qk_hi, 1)
                elif step == "V":
                    act.wait_ge(proj, PROJ_BANK[step, g, u] + 1)
                    nc.scalar.copy(vv[:, g * NT + u, :, 0:HD],
                                   proj_bank[PROJ_BANK[step, g, u] % 4][:, 0:D].rearrange("p (h d) -> p h d", h=H)).then_inc(v_done, 1)
                elif step == "GH":
                    if u == 0:
                        act.wait_ge(ld_gu, 16)
                        act.wait_ge(filled[0], 256)
                        act.wait_ge(filled[1], 128)
                        act.wait_ge(filled[2], 128)
                    k, cols = u // 6, slice(u % 6 * 256, u % 6 * 256 + 256)
                    nc.scalar.copy(gu_hi[:, k, cols], gu_raw[:, k, cols]).then_inc(gu_hi_done, 1)
                elif step == "NM":
                    act.wait_ge(nm_t, g + 1)
                    if g >= 1:
                        act.wait_ge(nm_in, 32 * g)
                    nc.scalar.mul(nm[0][:, :], nm_bank[0:QH * NT, 0:P], -1.0).then_inc(nm_hi, 1)
                elif step == "S2":
                    j, heads = UNITS2[u]
                    w = S - P * j
                    n = NU * g + u
                    act.wait_ge(s2, n + 1)
                    if g >= 2 and u == 0:
                        act.wait_ge(pv, NT * (g - 1))
                    nc.scalar.activation(pt[:, g % 2, heads[0]:heads[-1] + 1, SEG[j]:SEG[j] + w],
                                         s2_bank[n % 2][:, 0:w * len(heads)].rearrange("p (h n) -> p h n", h=len(heads)),
                                         ACT.Exp, scale=SCALE).then_inc(exp_done, 1)
                elif step == "OC":
                    act.wait_ge(pv, NT * (g + 1))
                    if g >= 2:
                        act.wait_ge(m_full, MISC["OT", g - 2, 0] + 1)
                    nc.scalar.copy(ot[:, g % 2, :], pv_bank[:, :]).then_inc(ot_copied, 1)
                elif step == "OTR":
                    act.wait_ge(m_full, MISC[step, g, u] + 1)
                    if g == 0 and u == 0:
                        act.wait_ge(consts, CONSTS_ALL)
                    nc.scalar.copy(attnT[:, u, :], misc[:, :]).then_inc(m_read, 1)
                elif step == "XT":
                    act.wait_ge(m_full, MISC[step, g, u] + 1)
                    nc.scalar.copy(x1T[:, 0, g, u, :], misc[:, :]).then_inc(x1T_hi, 1)
                elif step == "RL":
                    act.wait_ge(m_full, MISC[step, g, u] + 1)
                    nc.scalar.copy(lgT[:, :], misc[0:2 * E, :]).then_inc(m_read, 1)
                elif step == "RT":
                    act.wait_ge(gap_done, g + 1)
                    nc.scalar.activation(th[:, :], gap[:, :], ACT.Tanh, scale=0.5).then_inc(th_done, 1)
                elif step == "GU":
                    n = FC * g + u
                    act.wait_ge(gate, n + 1)
                    if n == 0:
                        act.wait_ge(pv, NT * (G - 1))
                    if n >= 2:
                        act.wait_ge(gated_done, n - 1)
                    nc.scalar.activation(silu_g[:, n % 2, :], gate_bank(n)[:, :], ACT.Silu).then_inc(silu_done, 1)
                elif step == "CB":
                    n = FC * g + u
                    act.wait_ge(hid, n + 1)
                    if n >= 3:
                        act.wait_ge(down, 2 * (n - 2))
                    nc.scalar.copy(h_hl[:, n % 3, 0, :], hidden[:, n % 2, :]).then_inc(hid_hi, 1)

        @block.vector
        def _(dve):
            own = 0

            def then(ins):
                nonlocal own
                own += 1
                ins.then_inc(dve_own, 1)
                dve.wait_ge(dve_own, own)

            def norm_stats(n):
                then(nc.vector.bn_stats(stats[:, n, :], x[:, n % (B * NT), :]))
                nc.vector.bn_aggr(mv[:, n, :], stats[:, n, :]).then_inc(stat_done, 1)

            def norm_apply(n):
                dve.wait_ge(rstd_done, n // 2 + 1)
                for i in range(n, n + 2):
                    t = i % (B * NT)
                    last = nc.vector.tensor_scalar(x[:, t, :], x[:, t, :], mv[:, i, 0:1], rstd[:, i:i + 1],
                                                   ALU.subtract, ALU.mult)
                last.then_inc(ln_done, 1)

            for step, g, u in PLAN:
                if step == "PROJ":
                    n = PROJ_BANK[step, g, u]
                    side = 2 * (u % 2)
                    dve.wait_ge(qk_hi, 4 * g + u + 1)
                    nc.vector.tensor_tensor(qk[g][:, side + 1, u // 2, :], proj_bank[n % 4][:, :],
                                            qk[g][:, side, u // 2, :].bitcast(F32), ALU.subtract).then_inc(qk_lo, 1)
                elif step == "S1":
                    t, heads = UNITS1[u]
                    w = P * (t + 1)
                    n = NU * g + u
                    dve.wait_ge(s1, n + 1)
                    nc.vector.tensor_reduce(mx[:, g % 2, heads[0]:heads[-1] + 1, t],
                                            s1_bank[n % 3][:, 0:w * len(heads)].rearrange("p (h n) -> p h n", h=len(heads)),
                                            AX.X, ALU.max).then_inc(s1_read, 1)
                elif step == "NM":
                    dve.wait_ge(nm_hi, g + 1)
                    nc.vector.scalar_tensor_tensor(out=nm[1][:, :], in0=nm_bank[0:QH * NT, 0:P], scalar=-1.0,
                                                   in1=nm[0][:, :].bitcast(F32), op0=ALU.mult,
                                                   op1=ALU.subtract).then_inc(nm_lo, 1)
                elif step == "OT":
                    m = misc[:, :].rearrange("p (t h c) -> p t h c", t=NT, h=QH)
                    dve.wait_ge(m_full, MISC[step, g, u] + 1)
                    if g == NQ:
                        dve.wait_ge(m_full, MISC["OTR", 0, 1] + 1)
                    then(nc.vector.reciprocal(rden[:, g % 2], m[:, :, :, HD]))
                    q = g % NQ
                    o = attn[:, :, q * 64:q * 64 + 64].rearrange("p t (h d) -> p t h d", h=QH)
                    nc.vector.tensor_tensor(o, m[:, :, :, 0:HD], rden[:, g % 2].unsqueeze(3).to_broadcast([P, NT, QH, HD]),
                                            ALU.mult).then_inc(attn_done, 1)
                    dve.wait_ge(attn_done, g + 1)
                    dve.sem_inc(m_read, 1)
                elif step == "Y":
                    dve.wait_ge(m_full, MISC[step, g, u] + 1)
                    if g == 0 and u == 0:
                        dve.wait_ge(ld_x, 16)
                    t = g * NT + 2 * u
                    own_x = x[:, t:t + 2, :].rearrange("p t n -> p (t n)")
                    nc.vector.tensor_tensor(own_x, misc[:, :], own_x, ALU.add).then_inc(m_read, 1)
                    dve.wait_ge(m_read, MISC[step, g, u] + 1)
                    norm_stats(t)
                    norm_stats(t + 1)
                elif step == "LN1":
                    norm_apply(NT * g)
                    norm_apply(NT * g + 2)
                elif step == "LN2":
                    for m in range(2):
                        dve.wait_ge(down, 2 * (FC * g + FC - 1) + m + 1)
                        t = g * NT + 2 * m
                        own_x = x[:, t:t + 2, :].rearrange("p t n -> p (t n)")
                        nc.vector.tensor_tensor(own_x, y_bank[m][:, :], own_x, ALU.add).then_inc(y_read, 1)
                        dve.wait_ge(y_read, 2 * g + m + 1)
                        norm_stats(B * NT + t)
                        norm_stats(B * NT + t + 1)
                    norm_apply(NT * (B + g))
                    norm_apply(NT * (B + g) + 2)
                elif step == "XT":
                    dve.wait_ge(x1T_hi, KC * g + u + 1)
                    nc.vector.tensor_tensor(x1T[:, 1, g, u, :], misc[:, :], x1T[:, 0, g, u, :].bitcast(F32),
                                            ALU.subtract).then_inc(x1T_done, 1)
                    dve.wait_ge(x1T_done, KC * g + u + 1)
                    dve.sem_inc(m_read, 1)
                elif step == "RT":
                    m = misc[:, 0:NT * 2 * E].rearrange("p (t n) -> p t n", t=NT)
                    dve.wait_ge(m_full, MISC[step, g, u] + 1)
                    then(nc.vector.tensor_copy(lg2[:, :, :], m[:, :, E:2 * E]))
                    nc.vector.tensor_tensor(lg[:, :, :], m[:, :, 0:E], lg2[:, :, :], ALU.add).then_inc(m_read, 1)
                    dve.wait_ge(m_read, MISC[step, g, u] + 1)
                    for t in range(NT):
                        last = nc.vector.max(top[:, t, :], lg[:, t, :])
                    then(last)
                    for t in range(NT):
                        last = nc.vector.max_index(topi[:, t, :], top[:, t, :], lg[:, t, :])
                    then(last)
                    then(nc.vector.tensor_copy(topf[:, :, :], topi[:, :, 0:2]))
                    nc.vector.tensor_tensor(gap[:, :], top[:, :, 0], top[:, :, 1], ALU.subtract).then_inc(gap_done, 1)
                    dve.wait_ge(th_done, g + 1)
                    nc.vector.tensor_scalar(wsel[:, :, 0], th[:, :], 0.5, 0.5, ALU.mult, ALU.add)
                    then(nc.vector.tensor_scalar(wsel[:, :, 1], th[:, :], -0.5, 0.5, ALU.mult, ALU.add))
                    if g == 0:
                        dve.wait_ge(consts, CONSTS_ALL)
                    for t in range(NT):
                        nc.vector.tensor_scalar(c1[:, t, :], iota_e[:, :], topf[:, t, 0:1], wsel[:, t, 0:1],
                                                ALU.is_equal, ALU.mult)
                        last = nc.vector.tensor_scalar(coef[:, t, :], iota_e[:, :], topf[:, t, 1:2], wsel[:, t, 1:2],
                                                       ALU.is_equal, ALU.mult)
                    then(last)
                    then(nc.vector.tensor_tensor(coef[:, :, :], coef[:, :, :], c1[:, :, :], ALU.add))
                    then(nc.vector.tensor_copy(coefhl[:, :, 0:E].bitcast(F32R), coef[:, :, :]))
                    nc.vector.tensor_tensor(coefhl[:, :, E:2 * E], coef[:, :, :], coefhl[:, :, 0:E],
                                            ALU.subtract).then_inc(coef_done, 1)
                elif step == "RC":
                    dve.wait_ge(m_full, MISC[step, g, u] + 1)
                    nc.vector.tensor_copy(coefT[:, g, :], misc[0:2 * E, :]).then_inc(coefT_done, 1)
                    dve.wait_ge(coefT_done, g + 1)
                    dve.sem_inc(m_read, 1)
                elif step == "GU":
                    n = FC * g + u
                    dve.wait_ge(silu_done, n + 1)
                    if n >= 3:
                        dve.wait_ge(hid, n - 2)
                    dve.wait_ge(up, n + 1)
                    nc.vector.tensor_tensor(gated[:, n % 3, :], up_bank(n)[:, :], silu_g[:, n % 2, :],
                                            ALU.mult).then_inc(gated_done, 1)
                elif step == "CB":
                    n = FC * g + u
                    dve.wait_ge(coefs, n + 1)
                    dve.wait_ge(gated_done, n + 1)
                    nc.vector.tensor_tensor(hidden[:, n % 2, :], coef_bank[:, :], gated[:, n % 3, :],
                                            ALU.mult).then_inc(hid, 1)
                elif step == "HL":
                    n = FC * g + u
                    dve.wait_ge(hid_hi, n + 1)
                    nc.vector.tensor_tensor(h_hl[:, n % 3, 1, :], hidden[:, n % 2, :], h_hl[:, n % 3, 0, :].bitcast(F32),
                                            ALU.subtract).then_inc(hid_lo, 1)

        @block.tensor
        def _(pe):
            def misc_free(step):
                if MISC[step] >= 1:
                    pe.wait_ge(m_read, MISC[step])

            for step, g, u in PLAN:
                if step in ("PROJ", "V"):
                    n = PROJ_BANK[step, g, u]
                    if g == 0 and (step == "PROJ" and u < 2 or step == "V" and u == 0):
                        pe.wait_ge(ld_w[1 - u % 2 if step == "PROJ" else 2], 16)
                    if n == 0 or step == "PROJ" and g == 1 and u == 0:
                        pe.wait_ge(ld_xT[g], 16)
                    before = [s for s, m in PROJ_BANK.items() if m == n - 4]
                    if before and before[0][0] == "PROJ":
                        pe.wait_ge(qk_lo, 4 * before[0][1] + before[0][2] + 1)
                    elif before:
                        pe.wait_ge(v_done, 4 * before[0][1] + before[0][2] + 1)
                    for k in range(KC):
                        if step == "PROJ":
                            c = u // 2
                            last = nc.tensor.matmul(proj_bank[n % 4][:, :], wqkv[:, 1 - u % 2, k, c * P:c * P + P],
                                                    xT[:, k, g * S:g * S + S], start=(k == 0), stop=(k == KC - 1))
                        else:
                            last = nc.tensor.matmul(proj_bank[n % 4][:, 0:D], xT[:, k, g * S + u * P:g * S + u * P + P],
                                                    wqkv[:, 2, k, :], start=(k == 0), stop=(k == KC - 1))
                    last.then_inc(proj, 1)
                elif step == "S1":
                    t, heads = UNITS1[u]
                    w = P * (t + 1)
                    n = NU * g + u
                    if u == 0:
                        pe.wait_ge(filled[g % SLOTS], 128 * (g // SLOTS + 1))
                    if n == 0:
                        pe.wait_ge(consts, CONSTS)
                    if n >= 3:
                        pe.wait_ge(s1_read, n - 2)
                    for m, h in enumerate(heads):
                        nc.tensor.matmul(s1_bank[n % 3][:, m * w:m * w + w], stacks[0:MAXROW, g % SLOTS, 1, h, t * P:t * P + P],
                                         stacks[0:MAXROW, g % SLOTS, 0, h, 0:w], start=True, stop=False)
                        last = nc.tensor.matmul(s1_bank[n % 3][:, m * w + w - P:m * w + w], identb[:, :], maskb[:, :],
                                                start=False, stop=True)
                    last.then_inc(s1, 1)
                elif step == "NM":
                    pe.wait_ge(s1_read, NU * (g + 1))
                    if g == 0:
                        pe.wait_ge(qk_lo, 8)
                        pe.wait_ge(v_done, 8)
                    else:
                        pe.wait_ge(nm_lo, g)
                    nc.tensor.transpose(nm_bank[0:QH * NT, 0:P], mx[:, g % 2].rearrange("p h t -> p (h t)"),
                                        ident[:, :]).then_inc(nm_t, 1)
                elif step == "S2":
                    j, heads = UNITS2[u]
                    w = S - P * j
                    n = NU * g + u
                    if u == 0:
                        pe.wait_ge(nm_in, 32 * (g + 1))
                    if n >= 2:
                        pe.wait_ge(exp_done, n - 1)
                    for m, h in enumerate(heads):
                        last = nc.tensor.matmul(s2_bank[n % 2][:, m * w:m * w + w],
                                                stacks[0:MAXROW + 2, g % SLOTS, 0, h, j * P:j * P + P],
                                                stacks[0:MAXROW + 2, g % SLOTS, 1, h, j * P:S], start=True, stop=True)
                    last.then_inc(s2, 1)
                elif step == "PV":
                    j = u
                    pe.wait_ge(masked, NT * g + j + 1)
                    if g >= 1 and j == 0:
                        pe.wait_ge(ot_copied, g)
                    for h in range(QH):
                        last = nc.tensor.matmul(pv_bank[32 * h:32 * h + VW, j * P:S],
                                                vv[:, g // NQ * NT + j, g % NQ * QH + h, :],
                                                pt[:, g % 2, h, SEG[j]:SEG[j] + S - P * j],
                                                start=(j == 0), stop=(j == NT - 1))
                    last.then_inc(pv, 1)
                elif step == "OT":
                    misc_free((step, g, u))
                    pe.wait_ge(ot_copied, g + 1)
                    for t in range(NT):
                        last = nc.tensor.transpose(misc[:, t * P:t * P + P], ot[:, g % 2, t * P:t * P + P], ident[:, :])
                    last.then_inc(m_full, 1)
                elif step == "OTR":
                    misc_free((step, g, u))
                    pe.wait_ge(attn_done, NQ * (g + 1))
                    for t in range(NT):
                        last = nc.tensor.transpose(misc[:, t * P:t * P + P], attn[:, t, u * P:u * P + P], ident[:, :])
                    last.then_inc(m_full, 1)
                elif step == "Y":
                    misc_free((step, g, u))
                    pe.wait_ge(ld_wp, 16)
                    for m in range(2):
                        t = 2 * u + m
                        for k in range(KC):
                            last = nc.tensor.matmul(misc[:, m * D:m * D + D], attnT[:, k, t * P:t * P + P], wp[:, k, :],
                                                    start=(k == 0), stop=(k == KC - 1))
                    last.then_inc(m_full, 1)
                elif step == "XT":
                    misc_free((step, g, u))
                    pe.wait_ge(ln_done, 2 * (g + 1))
                    for t in range(NT):
                        last = nc.tensor.transpose(misc[:, t * P:t * P + P], x[:, g * NT + t, u * P:u * P + P], ident[:, :])
                    last.then_inc(m_full, 1)
                elif step == "RL":
                    misc_free((step, g, u))
                    pe.wait_ge(x1T_done, KC * (g + 1))
                    pe.wait_ge(consts, CONSTS_ALL)
                    for k in range(KC):
                        for part in (1, 0):
                            last = nc.tensor.matmul(misc[0:2 * E, :], wr[:, k, :], x1T[:, part, g, k, :],
                                                    start=(k == 0 and part == 1), stop=(k == KC - 1 and part == 0))
                    last.then_inc(m_full, 1)
                elif step == "RT":
                    misc_free((step, g, u))
                    for t in range(NT):
                        last = nc.tensor.transpose(misc[:, t * 2 * E:t * 2 * E + 2 * E], lgT[:, t * P:t * P + P],
                                                   ident[0:2 * E, 0:2 * E])
                    last.then_inc(m_full, 1)
                elif step == "RC":
                    misc_free((step, g, u))
                    pe.wait_ge(coef_done, g + 1)
                    for t in range(NT):
                        last = nc.tensor.transpose(misc[0:2 * E, t * P:t * P + P], coefhl[:, t, :], ident[:, :])
                    last.then_inc(m_full, 1)
                elif step == "GU":
                    n = FC * g + u
                    if n == 0:
                        pe.wait_ge(gu_split, KC * 6)
                        pe.wait_ge(s1_read, NU * G)
                    if u == 0:
                        pe.wait_ge(x1T_done, KC * (g + 1))
                    for dst, col, done in ((gate_bank(n), u * P, gate), (up_bank(n), EI + u * P, up)):
                        if done is gate and n >= 2:
                            pe.wait_ge(gated_done, n - 1)
                        if done is up and n >= 1:
                            pe.wait_ge(silu_done, n)
                        for k in range(KC):
                            for w, part in ((gu_lo, 0), (gu_hi, 1), (gu_hi, 0)):
                                last = nc.tensor.matmul(dst[:, :], w[:, k, col:col + P], x1T[:, part, g, k, :],
                                                        start=(k == 0 and w is gu_lo), stop=(k == KC - 1 and w is gu_hi and part == 0))
                        last.then_inc(done, 1)
                elif step == "CB":
                    n = FC * g + u
                    if n == 0:
                        pe.wait_ge(nm_lo, G)
                    if u == 0:
                        pe.wait_ge(coefT_done, g + 1)
                    if n >= 1:
                        pe.wait_ge(hid, n)
                    nc.tensor.matmul(coef_bank[:, :], spread_r[:, u * P:u * P + P], coefT[:, g, :],
                                     start=True, stop=True).then_inc(coefs, 1)
                elif step == "DN":
                    n = FC * g + u
                    pe.wait_ge(hid_hi, n + 1)
                    pe.wait_ge(hid_lo, n + 1)
                    if n == 0:
                        pe.wait_ge(wd_split, FC)
                        pe.wait_ge(exp_done, NU * G)
                    if u == 0 and g >= 1:
                        pe.wait_ge(y_read, 2 * g)
                    for t in range(NT):
                        for part, w in ((1, 0), (0, 1), (0, 0)):
                            last = nc.tensor.matmul(y_bank[t // 2][:, t % 2 * D:t % 2 * D + D],
                                                    h_hl[:, n % 3, part, t * P:t * P + P], wd_hl[:, w, u, :],
                                                    start=(u == 0 and t % 2 == 0 and part == 1),
                                                    stop=(u == FC - 1 and part == 0 and w == 0), skip_group_check=True)
                        if t % 2:
                            last.then_inc(down, 1)


def kernel(L0_attn_x, L0_attn_Wq, L0_attn_Wk, L0_attn_Wv, L0_attn_Wp, L0_ffn_router_w, L0_ffn_gate_w, L0_ffn_up_w, L0_ffn_down_w):
    import numpy as np
    import concourse.bacc as bacc
    from concourse.bass_utils import run_bass_kernel_spmd

    def rows(a):
        return np.ascontiguousarray(a.reshape(-1, P, a.shape[1]).transpose(1, 0, 2))

    def by_group(w):
        return w.T.reshape(D, NQ, QH, HD).transpose(0, 1, 3, 2).reshape(D, D)

    x = np.asarray(L0_attn_x).reshape(B * S, D)
    wq, wk, wv, wp = (np.asarray(w) for w in (L0_attn_Wq, L0_attn_Wk, L0_attn_Wv, L0_attn_Wp))
    gate, up, down = (np.asarray(w) for w in (L0_ffn_gate_w, L0_ffn_up_w, L0_ffn_down_w))
    arrays = {
        "xT": rows(x.T), "x": rows(x),
        "wqkv": np.ascontiguousarray(np.stack([rows(by_group(wq)), rows(by_group(wk)), rows(wv.T)], axis=1)),
        "wp": rows(wp.T), "wr": rows(np.asarray(L0_ffn_router_w).T),
        "wgu": rows(np.concatenate([gate.reshape(EI, D).T, up.reshape(EI, D).T], axis=1)),
        "wd": rows(down.transpose(0, 2, 1).reshape(EI, D)),
    }
    nc = bacc.Bacc("TRN2", target_bir_lowering=False, num_devices=1)
    aps = [nc.dram_tensor(n + "_dram", a.shape, mybir.dt.from_np(a.dtype), kind="ExternalInput").ap() for n, a in arrays.items()]
    out = nc.dram_tensor("out_dram", [P, B * NT, D], F32, kind="ExternalOutput").ap()
    layer_kernel(nc, *aps, out)
    r = run_bass_kernel_spmd(nc, [{n + "_dram": a for n, a in arrays.items()}], core_ids=[0])
    return np.ascontiguousarray(r.results[0]["out_dram"].transpose(1, 0, 2)).reshape(B, S, D)
```

```python
from contextlib import ExitStack

import concourse.bass as bass
from concourse import mybir

F32 = mybir.dt.float32
F32R = mybir.dt.float32r
BF16 = mybir.dt.bfloat16
U32 = mybir.dt.uint32
ALU = mybir.AluOpType
ACT = mybir.ActivationFunctionType
AX = mybir.AxisListType

P = 128
B, S, D = 2, 512, 256
H, HD = 16, 16
KC = D // P
NT = S // P
QH = 4
NQ = H // QH
G = B * NQ
E, I = 8, 96
EI = E * I
FC = EI // P
EPS = 1e-5
SCALE = HD ** -0.5
MASKED = -1e30

PARTS = ((0, 1, 0), (2, 2, 3))
MAXROW = 96
SLOTS = 3
SEG = [0, 512, 896, 1152]
PTW = 1280
VW = 32

UNITS1 = [(3, [h]) for h in range(4)] + [(2, [h]) for h in range(4)] + [(1, [0, 1]), (1, [2, 3]), (0, [0, 1, 2, 3])]
UNITS2 = [(3 - t, hs) for t, hs in UNITS1]
NU = len(UNITS1)
MASK_MADE = 2
SLOT_MADE = [0, 4, 6]
CONSTS = 10
WARM = 8
CONSTS_ALL = CONSTS + E + 7
MASK_AFTER = [4, 8, 10, 11]


LEAD = NU + 5


def chain(b):
    return [("OTR", b, 0), ("OTR", b, 1), ("Y", b, 0), ("Y", b, 1), ("LN1", b, 0), ("XT", b, 0), ("XT", b, 1),
            ("RL", b, 0), ("RT", b, 0), ("RC", b, 0)]


def make_plan():
    plan = [("PROJ", 0, n) for n in range(4)] + [("V", 0, 0)]
    projections = {2: ("V", 0, 1), 5: ("PROJ", 1, 0), 9: ("PROJ", 1, 1), 13: ("PROJ", 1, 2),
                   LEAD + 4: ("PROJ", 1, 3), LEAD + 12: ("V", 1, 0), LEAD + 16: ("V", 1, 1)}
    links = []
    for s in range(G * NU + LEAD):
        if s < G * NU:
            plan.append(("S1", s // NU, s % NU))
        if s in projections:
            plan.append(projections[s])
        if s >= NU and s % NU == 0 and s <= G * NU:
            plan.append(("NM", s // NU - 1, 0))
        if s >= LEAD:
            g, u = divmod(s - LEAD, NU)
            plan.append(("S2", g, u))
            if g >= 1 and u in (2, 4, 6, 8):
                plan.append(("PV", g - 1, u // 2 - 1))
            if g >= 1 and u == 9:
                plan.append(("OC", g - 1, 0))
            if g >= 1 and u == 10:
                plan.append(("OT", g - 1, 0))
                if g == NQ:
                    links = chain(0)
            if links and u % 2 and u < 10:
                plan.append(links.pop(0))
            if g in (2, 3, 4) and u in (1, 3, 5, 7):
                plan.append(("GH", 0, 4 * (g - 2) + u // 2))
    plan += links
    links = chain(1)
    plan += [("GU", 0, 0)] + [("PV", G - 1, j) for j in range(NT)] + [("OC", G - 1, 0), ("GU", 0, 1), ("OT", G - 1, 0)]
    n_links = {2: (1, 1), 3: (1, 1), 4: (1, 0), 5: (1, 1), 6: (1, 1), 7: (1, 0)}
    for n in range(2, B * FC + 2):
        back = ((n - 2) // FC, (n - 2) % FC)
        plan += [("CB", *back), ("HL", *back)]
        if n < B * FC:
            plan.append(("GU", n // FC, n % FC))
        before, after = n_links.get(n, (0, 0))
        plan += [links.pop(0) for _ in range(before)]
        plan.append(("DN", *back))
        plan += [links.pop(0) for _ in range(after)]
        if back[1] == FC - 1:
            plan.append(("LN2", back[0], 0))
    assert not links
    return plan


PLAN = make_plan()
EARLY = {s: n for n, s in enumerate([s for s in PLAN[:PLAN.index(("S2", 0, 0))] if s[0] in ("PROJ", "V")])}
LATE = [s for s in PLAN if s[0] in ("PROJ", "V") and s not in EARLY]
EARLY_QK = sum(s[0] == "PROJ" for s in EARLY)
EARLY_V = len(EARLY) - EARLY_QK
MISC = {s: n for n, s in enumerate([s for s in PLAN if s in LATE or s[0] in ("OT", "OTR", "Y", "XT", "RL", "RT", "RC")])}


def layer_kernel(nc, xT_d, x_d, wqkv_d, wp_d, wr_d, wgu_d, wd_d, out_d):
    with ExitStack() as ctx:
        def sb(name, shape, dt=F32):
            return ctx.enter_context(nc.sbuf_tensor(name, shape, dt))

        def sem(name):
            return ctx.enter_context(nc.semaphore(name))

        early = sb("early", [P, 14 * 256])
        xT = early[:, 0:KC * B * S].rearrange("p (k n) -> p k n", k=KC)
        wqkv = early[:, KC * B * S:].rearrange("p (w k n) -> p w k n", w=3, k=KC)
        gu_raw = early[:, 0:KC * 2 * EI].rearrange("p (k n) -> p k n", k=KC)
        wp = sb("wp", [P, KC, D])
        wd_raw = sb("wd_raw", [P, FC, D])
        wr_raw = sb("wr_raw", [P, KC, E])
        wr = sb("wr", [P, KC, 2 * E], F32R)
        x = sb("x", [P, B * NT, D])
        qk = [sb(f"qk{b}", [P, 4, KC, S], F32R) for b in range(B)]
        gu_hi = qk[0][:, 0:3].rearrange("p a k n -> p (a k n)").rearrange("p (k n) -> p k n", k=KC)
        gu_lo = qk[1][:, 0:3].rearrange("p a k n -> p (a k n)").rearrange("p (k n) -> p k n", k=KC)
        vv = sb("vv", [P, B * NT, H, VW])
        stacks = sb("stacks", [P, SLOTS, 2, QH, S], F32R)
        flat = [stacks[:, n].rearrange("p a h n -> p (a h n)") for n in range(SLOTS)]
        h_hl = flat[0][:, 0:3 * 2 * S].rearrange("p (r a n) -> p r a n", r=3, a=2)
        wd_hl = flat[2][:, 0:2 * FC * D].rearrange("p (a c n) -> p a c n", a=2, c=FC)
        pt = sb("pt", [P, 2, QH, PTW])
        warm = pt[:, 1, 0, 0:S // 2].bitcast(BF16)
        temps = pt[:, 0].rearrange("p h n -> p (h n)")
        silu_g = temps[:, 0:2 * S].rearrange("p (r n) -> p r n", r=2)
        gated = temps[:, 2 * S:5 * S].rearrange("p (r n) -> p r n", r=3)
        hidden = temps[:, 5 * S:7 * S].rearrange("p (r n) -> p r n", r=2)
        ot = sb("ot", [P, 2, S])
        attn = sb("attn", [P, NT, D])
        attnT = sb("attnT", [P, KC, S])
        x1T = sb("x1T", [P, 2, B, KC, S], F32R)
        mx = sb("mx", [P, 2, QH, NT])
        nm = [sb("nm_hi", [QH * NT, P], F32R), sb("nm_lo", [QH * NT, P], F32R)]
        rden = sb("rden", [P, 2, NT, QH])
        stats = sb("stats", [P, 2 * B * NT, 6])
        mv = sb("mv", [P, 2 * B * NT, 2])
        var_eps = sb("var_eps", [P, 2 * B * NT])
        rstd = sb("rstd", [P, 2 * B * NT])
        lgT = sb("lgT", [2 * E, S])
        lg2 = sb("lg2", [P, NT, E])
        lg = sb("lg", [P, NT, E])
        top = sb("top", [P, NT, E])
        topi = sb("topi", [P, NT, E], U32)
        topf = sb("topf", [P, NT, 2])
        gap = sb("gap", [P, NT])
        th = sb("th", [P, NT])
        wsel = sb("wsel", [P, NT, 2])
        c1 = sb("c1", [P, NT, E])
        coef = sb("coef", [P, NT, E])
        coefhl = sb("coefhl", [P, NT, 2 * E])
        coefT = qk[0][0:2 * E, 3, :, :]
        ident = sb("ident", [P, P])
        mask = sb("mask", [P, S], BF16)
        spread = attnT[0:2 * E].rearrange("p k n -> p (k n)")[:, 0:EI]
        spread_r = sb("spread_r", [2 * E, EI], F32R)
        iota_e = sb("iota_e", [P, E])
        minus_half = sb("minus_half", [P, 2])

        bank = [ctx.enter_context(nc.psum_tensor(f"bank{n}", [P, 512], F32)) for n in range(8)]
        s1_bank, s2_bank, pv_bank, nm_bank, misc = bank[0:3], bank[3:5], bank[5], bank[6], bank[7]
        proj_bank = bank[3:6]
        ffn_bank, coef_bank, y_bank = bank[0:3], bank[6], bank[3:5]

        def gate_bank(n):
            return ffn_bank[2 * n % 3]

        def up_bank(n):
            return ffn_bank[(2 * n + 1) % 3]

        ld_xT = [sem(n) for n in ("ld_xT0_k0", "ld_xT0_k1", "ld_xT1")]
        ld_wp, ld_x, ld_wr, ld_gu, ld_wd = (sem(n) for n in ("ld_wp", "ld_x", "ld_wr", "ld_gu", "ld_wd"))
        ld_w = [sem(f"ld_w{n}") for n in "qkv"]
        consts = sem("consts")
        pool_own = sem("pool_own")
        proj = sem("proj")
        qk_hi = sem("qk_hi")
        qk_lo = sem("qk_lo")
        v_done = sem("v_done")
        warm_set = sem("warm_set")
        slot0_set = sem("slot0_set")
        filled = [sem(f"filled{n}") for n in range(SLOTS)]
        s1 = sem("s1")
        s1_read = sem("s1_read")
        nm_t = sem("nm_t")
        nm_hi = sem("nm_hi_done")
        nm_lo = sem("nm_lo_done")
        nm_in = sem("nm_in")
        s2 = sem("s2")
        exp_done = sem("exp_done")
        masked = sem("masked")
        pv = sem("pv")
        ot_copied = sem("ot_copied")
        m_full = sem("m_full")
        m_read = sem("m_read")
        dve_own = sem("dve_own")
        attn_done = sem("attn_done")
        attnT_done = sem("attnT_done")
        stat_done = sem("stat_done")
        rstd_done = sem("rstd_done")
        ln_done = sem("ln_done")
        x1T_hi = sem("x1T_hi")
        x1T_done = sem("x1T_done")
        lgT_done = sem("lgT_done")
        gap_done = sem("gap_done")
        th_done = sem("th_done")
        coef_done = sem("coef_done")
        coefT_done = sem("coefT_done")
        gu_hi_done = sem("gu_hi_done")
        gu_split = sem("gu_split")
        wd_split = sem("wd_split")
        gate = sem("gate")
        up = sem("up")
        coefs = sem("coefs")
        silu_done = sem("silu_done")
        gated_done = sem("gated_done")
        hid = sem("hid")
        hid_hi = sem("hid_hi")
        hid_lo = sem("hid_lo")
        down = sem("down")
        y_read = sem("y_read")
        stored = sem("stored")

        def projected(eng, step):
            if step in EARLY:
                eng.wait_ge(proj, EARLY[step] + 1)
                return proj_bank[EARLY[step] % 3]
            eng.wait_ge(m_full, MISC[step] + 1)
            return misc

        block = ctx.enter_context(nc.Block())

        @block.sync
        def _(sp):
            for k in range(KC):
                sp.dma_start(xT[:, k, 0:S], xT_d[:, k, 0:S]).then_inc(ld_xT[k], 16)
            sp.dma_start(wqkv[:, 2], wqkv_d[:, 2]).then_inc(ld_w[2], 16)
            sp.dma_start(xT[:, :, S:2 * S], xT_d[:, :, S:2 * S]).then_inc(ld_xT[KC], 16)

            def fill(g):
                b, c, r = g // NQ, g % NQ // 2, 64 * (g % 2)
                if g >= SLOTS:
                    sp.wait_ge(s2, NU * (g - SLOTS + 1))
                elif g == 0:
                    sp.wait_ge(slot0_set, 3)
                else:
                    sp.wait_ge(consts, SLOT_MADE[g])
                for part in range(4):
                    sp.wait_ge(qk_lo if part % 2 else qk_hi, 4 * b + 2 * c + part // 2 + 1)
                    for n in range(3):
                        if PARTS[part // 2][n] == part:
                            sp.dma_start(stacks[HD * n:HD * n + HD, g % SLOTS, part // 2, :, :].bitcast(F32),
                                         qk[b][r:r + 64, part, c, :].bitcast(F32)).then_inc(filled[g % SLOTS], 16)

            fill(0)
            fill(1)
            fill(2)
            sp.dma_start(x[:, :, :], x_d).then_inc(ld_x, 16)
            sp.dma_start(wp[:, :, :], wp_d).then_inc(ld_wp, 16)
            sp.dma_start(wr_raw[:, :, :], wr_d).then_inc(ld_wr, 16)
            sp.dma_start(wd_raw[:, :, :], wd_d).then_inc(ld_wd, 16)
            for step, g, u in PLAN:
                if step == "NM":
                    sp.wait_ge(nm_hi, g + 1)
                    sp.wait_ge(nm_lo, g + 1)
                    for n in range(2):
                        sp.dma_start(stacks[MAXROW + n:MAXROW + n + 1, g % SLOTS, 1, :, :].bitcast(F32),
                                     nm[n][:, :].bitcast(F32)).then_inc(nm_in, 16)
                    if g == 2:
                        sp.wait_ge(m_full, MISC[LATE[-1]] + 1)
                        sp.dma_start(gu_raw, wgu_d).then_inc(ld_gu, 16)
                if step == "S2" and u == NU - 1 and g + SLOTS < G:
                    fill(g + SLOTS)
                if step == "LN2":
                    for t in range(g * NT, g * NT + NT, 2):
                        sp.wait_ge(ln_done, (B * NT + t) // 2 + 1)
                        sp.dma_start(out_d[:, t:t + 2, :], x[:, t:t + 2, :]).then_inc(stored, 16)
            sp.wait_ge(stored, 16 * B * NT // 2)

        @block.gpsimd
        def _(pool):
            made = 0

            def make(ins):
                nonlocal made
                made += 1
                ins.then_inc(consts, 1)
                pool.wait_ge(consts, made)

            make(nc.gpsimd.memset(mask[:, :], 0.0))
            make(nc.gpsimd.affine_select(out=mask[:, S - P:S], in_=mask[:, S - P:S], compare_op=ALU.is_ge, fill=MASKED, base=0,
                                         pattern=[[-1, P]], channel_multiplier=1))
            assert made == MASK_MADE
            for n in range(1, SLOTS):
                make(nc.gpsimd.memset(stacks[0:MAXROW, n].bitcast(F32), 0.0))
                make(nc.gpsimd.memset(stacks[MAXROW:MAXROW + 2, n, 0].bitcast(F32), 1.0))
                assert made == SLOT_MADE[n]
            make(nc.gpsimd.memset(ident[:, :], 0.0))
            make(nc.gpsimd.affine_select(out=ident[:, :], in_=ident[:, :], compare_op=ALU.not_equal, fill=1.0, base=0,
                                         pattern=[[-1, P]], channel_multiplier=1))
            make(nc.gpsimd.memset(vv[:, :, :, HD:HD + 1], 1.0))
            make(nc.gpsimd.memset(vv[:, :, :, HD + 1:VW], 0.0))
            assert made == CONSTS
            make(nc.gpsimd.memset(minus_half[:, :], -0.5))
            for e in range(E):
                make(nc.gpsimd.memset(iota_e[:, e:e + 1], float(e)))
            make(nc.gpsimd.memset(spread[:, :], 0.0))
            for n in range(2):
                v = spread[:, :].rearrange("p (e i) -> p e i", e=E)
                make(nc.gpsimd.affine_select(out=v, in_=v, compare_op=ALU.not_equal, fill=1.0, base=-E * n,
                                             pattern=[[-1, E], [0, I]], channel_multiplier=1))
            make(nc.gpsimd.tensor_copy(spread_r[:, :], spread[:, :]))
            pool.wait_ge(ld_wr, 16)
            make(nc.gpsimd.tensor_copy(wr[:, :, 0:E], wr_raw[:, :, :]))
            make(nc.gpsimd.tensor_tensor(wr[:, :, E:2 * E], wr_raw[:, :, :], wr[:, :, 0:E].bitcast(F32), ALU.subtract))
            assert made == CONSTS_ALL
            own = 0

            def then(ins):
                nonlocal own
                own += 1
                ins.then_inc(pool_own, 1)
                pool.wait_ge(pool_own, own)


            for step, g, u in PLAN:
                if step == "S2" and u + 1 in MASK_AFTER:
                    j = MASK_AFTER.index(u + 1)
                    pool.wait_ge(exp_done, NU * g + u + 1)
                    v = pt[:, g % 2, :, SEG[j]:SEG[j] + P]
                    nc.gpsimd.affine_select(out=v, in_=v, compare_op=ALU.is_ge, fill=0.0, base=0,
                                            pattern=[[0, QH], [1, P]], channel_multiplier=-1).then_inc(masked, 1)
                    if g == 5 and j == 0:
                        for n in range(SLOTS):
                            pool.wait_ge(filled[n], 96 * ((G - 1 - n) // SLOTS + 1))
                    for n in range(2 * j, 2 * j + 2) if g == 5 else range(8 + j, 9 + j) if g == 6 else ():
                        k, cols = n // 6, slice(n % 6 * 256, n % 6 * 256 + 256)
                        pool.wait_ge(gu_hi_done, n + 1)
                        nc.gpsimd.tensor_tensor(gu_lo[:, k, cols], gu_raw[:, k, cols], gu_hi[:, k, cols].bitcast(F32),
                                                ALU.subtract).then_inc(gu_split, 1)
                    if g == G - 1 and j == NT - 1:
                        pool.wait_ge(ld_wd, 16)
                        for c in range(FC):
                            then(nc.gpsimd.tensor_copy(wd_hl[:, 0, c, :], wd_raw[:, c, :]))
                            nc.gpsimd.tensor_tensor(wd_hl[:, 1, c, :], wd_raw[:, c, :], wd_hl[:, 0, c, :].bitcast(F32),
                                                    ALU.subtract).then_inc(wd_split, 1)
                if step == "LN1" or step == "LN2":
                    first = NT * g if step == "LN1" else NT * (B + g)
                    for n in range(first, first + NT, 2):
                        pool.wait_ge(stat_done, n + 2)
                        then(nc.gpsimd.tensor_scalar(var_eps[:, n:n + 2], mv[:, n:n + 2, 1], EPS, None, ALU.add))
                        nc.gpsimd.tensor_tensor(rstd[:, n:n + 2], var_eps[:, n:n + 2], minus_half[:, :],
                                                ALU.pow).then_inc(rstd_done, 1)

        @block.scalar
        def _(act):
            act.dma_start(wqkv[:, 1], wqkv_d[:, 1]).then_inc(ld_w[1], 16)
            act.dma_start(wqkv[:, 0], wqkv_d[:, 0]).then_inc(ld_w[0], 16)
            for step, g, u in PLAN:
                if step == "PROJ":
                    src = projected(act, (step, g, u))
                    nc.scalar.copy(qk[g][:, 2 * (u % 2), u // 2, :], src[:, :]).then_inc(qk_hi, 1)
                elif step == "V":
                    src = projected(act, (step, g, u))
                    t = g * NT + 2 * u
                    nc.scalar.copy(vv[:, t:t + 2, :, 0:HD],
                                   src[:, :].rearrange("p (t h d) -> p t h d", t=2, h=H)).then_inc(v_done, 1)
                    if (step, g, u) in LATE:
                        act.wait_ge(v_done, 2 * g + u + 1)
                        act.sem_inc(m_read, 1)
                elif step == "GH":
                    if u == 0:
                        act.wait_ge(ld_gu, 16)
                        act.wait_ge(filled[0], 192)
                        act.wait_ge(filled[1], 96)
                        act.wait_ge(filled[2], 96)
                    k, cols = u // 6, slice(u % 6 * 256, u % 6 * 256 + 256)
                    nc.scalar.copy(gu_hi[:, k, cols], gu_raw[:, k, cols]).then_inc(gu_hi_done, 1)
                elif step == "NM":
                    act.wait_ge(nm_t, g + 1)
                    if g >= 1:
                        act.wait_ge(nm_in, 32 * g)
                    nc.scalar.mul(nm[0][:, :], nm_bank[0:QH * NT, 0:P], -1.0).then_inc(nm_hi, 1)
                elif step == "S2":
                    j, heads = UNITS2[u]
                    w = S - P * j
                    n = NU * g + u
                    act.wait_ge(s2, n + 1)
                    if g >= 2 and u == 0:
                        act.wait_ge(pv, NT * (g - 1))
                    nc.scalar.activation(pt[:, g % 2, heads[0]:heads[-1] + 1, SEG[j]:SEG[j] + w],
                                         s2_bank[n % 2][:, 0:w * len(heads)].rearrange("p (h n) -> p h n", h=len(heads)),
                                         ACT.Exp, scale=SCALE).then_inc(exp_done, 1)
                elif step == "OC":
                    act.wait_ge(pv, NT * (g + 1))
                    if g >= 2:
                        act.wait_ge(m_full, MISC["OT", g - 2, 0] + 1)
                    nc.scalar.copy(ot[:, g % 2, :], pv_bank[:, :]).then_inc(ot_copied, 1)
                elif step == "OTR":
                    act.wait_ge(m_full, MISC[step, g, u] + 1)
                    if g == 0 and u == 0:
                        act.wait_ge(consts, CONSTS_ALL)
                    nc.scalar.copy(attnT[:, u, :], misc[:, :]).then_inc(m_read, 1)
                elif step == "XT":
                    act.wait_ge(m_full, MISC[step, g, u] + 1)
                    nc.scalar.copy(x1T[:, 0, g, u, :], misc[:, :]).then_inc(x1T_hi, 1)
                elif step == "RL":
                    act.wait_ge(m_full, MISC[step, g, u] + 1)
                    nc.scalar.copy(lgT[:, :], misc[0:2 * E, :]).then_inc(m_read, 1)
                elif step == "RT":
                    act.wait_ge(gap_done, g + 1)
                    nc.scalar.activation(th[:, :], gap[:, :], ACT.Tanh, scale=0.5).then_inc(th_done, 1)
                elif step == "GU":
                    n = FC * g + u
                    act.wait_ge(gate, n + 1)
                    if n == 0:
                        act.wait_ge(pv, NT * (G - 1))
                    if n >= 2:
                        act.wait_ge(gated_done, n - 1)
                    nc.scalar.activation(silu_g[:, n % 2, :], gate_bank(n)[:, :], ACT.Silu).then_inc(silu_done, 1)
                elif step == "CB":
                    n = FC * g + u
                    act.wait_ge(hid, n + 1)
                    if n >= 3:
                        act.wait_ge(down, 2 * (n - 2))
                    nc.scalar.copy(h_hl[:, n % 3, 0, :], hidden[:, n % 2, :]).then_inc(hid_hi, 1)

        @block.vector
        def _(dve):
            own = 0

            def then(ins):
                nonlocal own
                own += 1
                ins.then_inc(dve_own, 1)
                dve.wait_ge(dve_own, own)

            def norm_stats(n):
                then(nc.vector.bn_stats(stats[:, n, :], x[:, n % (B * NT), :]))
                nc.vector.bn_aggr(mv[:, n, :], stats[:, n, :]).then_inc(stat_done, 1)

            def norm_apply(n):
                dve.wait_ge(rstd_done, n // 2 + 1)
                for i in range(n, n + 2):
                    t = i % (B * NT)
                    last = nc.vector.tensor_scalar(x[:, t, :], x[:, t, :], mv[:, i, 0:1], rstd[:, i:i + 1],
                                                   ALU.subtract, ALU.mult)
                last.then_inc(ln_done, 1)

            nc.vector.memset(warm[:, :], 0.0).then_inc(warm_set, 1)
            for side in range(2):
                nc.vector.memset(stacks[0:MAXROW, 0, side].bitcast(F32), 0.0).then_inc(slot0_set, 1)
            nc.vector.memset(stacks[MAXROW:MAXROW + 2, 0, 0].bitcast(F32), 1.0).then_inc(slot0_set, 1)
            for step, g, u in PLAN:
                if step == "PROJ":
                    side = 2 * (u % 2)
                    src = projected(dve, (step, g, u))
                    dve.wait_ge(qk_hi, 4 * g + u + 1)
                    nc.vector.tensor_tensor(qk[g][:, side + 1, u // 2, :], src[:, :],
                                            qk[g][:, side, u // 2, :].bitcast(F32), ALU.subtract).then_inc(qk_lo, 1)
                    if (step, g, u) in LATE:
                        dve.wait_ge(qk_lo, 4 * g + u + 1)
                        dve.sem_inc(m_read, 1)
                elif step == "S1":
                    t, heads = UNITS1[u]
                    w = P * (t + 1)
                    n = NU * g + u
                    dve.wait_ge(s1, n + 1)
                    if n == 0:
                        dve.wait_ge(consts, MASK_MADE)
                    for m, h in enumerate(heads):
                        scores = s1_bank[n % 3][:, m * w:m * w + w]
                        last = nc.vector.tensor_tensor_reduce(scores, scores, mask[:, S - w:S], 1.0, MASKED, ALU.add,
                                                              ALU.max, mx[:, g % 2, h, t:t + 1])
                    last.then_inc(s1_read, 1)
                elif step == "NM":
                    dve.wait_ge(nm_hi, g + 1)
                    nc.vector.scalar_tensor_tensor(out=nm[1][:, :], in0=nm_bank[0:QH * NT, 0:P], scalar=-1.0,
                                                   in1=nm[0][:, :].bitcast(F32), op0=ALU.mult,
                                                   op1=ALU.subtract).then_inc(nm_lo, 1)
                elif step == "OT":
                    m = misc[:, :].rearrange("p (t h c) -> p t h c", t=NT, h=QH)
                    dve.wait_ge(m_full, MISC[step, g, u] + 1)
                    if g == NQ:
                        dve.wait_ge(m_full, MISC["OTR", 0, 1] + 1)
                    then(nc.vector.reciprocal(rden[:, g % 2], m[:, :, :, HD]))
                    q = g % NQ
                    o = attn[:, :, q * 64:q * 64 + 64].rearrange("p t (h d) -> p t h d", h=QH)
                    nc.vector.tensor_tensor(o, m[:, :, :, 0:HD], rden[:, g % 2].unsqueeze(3).to_broadcast([P, NT, QH, HD]),
                                            ALU.mult).then_inc(attn_done, 1)
                    dve.wait_ge(attn_done, g + 1)
                    dve.sem_inc(m_read, 1)
                elif step == "Y":
                    dve.wait_ge(m_full, MISC[step, g, u] + 1)
                    if g == 0 and u == 0:
                        dve.wait_ge(ld_x, 16)
                    t = g * NT + 2 * u
                    own_x = x[:, t:t + 2, :].rearrange("p t n -> p (t n)")
                    nc.vector.tensor_tensor(own_x, misc[:, :], own_x, ALU.add).then_inc(m_read, 1)
                    dve.wait_ge(m_read, MISC[step, g, u] + 1)
                    norm_stats(t)
                    norm_stats(t + 1)
                elif step == "LN1":
                    norm_apply(NT * g)
                    norm_apply(NT * g + 2)
                elif step == "LN2":
                    for m in range(2):
                        dve.wait_ge(down, 2 * (FC * g + FC - 1) + m + 1)
                        t = g * NT + 2 * m
                        own_x = x[:, t:t + 2, :].rearrange("p t n -> p (t n)")
                        nc.vector.tensor_tensor(own_x, y_bank[m][:, :], own_x, ALU.add).then_inc(y_read, 1)
                        dve.wait_ge(y_read, 2 * g + m + 1)
                        norm_stats(B * NT + t)
                        norm_stats(B * NT + t + 1)
                    norm_apply(NT * (B + g))
                    norm_apply(NT * (B + g) + 2)
                elif step == "XT":
                    dve.wait_ge(x1T_hi, KC * g + u + 1)
                    nc.vector.tensor_tensor(x1T[:, 1, g, u, :], misc[:, :], x1T[:, 0, g, u, :].bitcast(F32),
                                            ALU.subtract).then_inc(x1T_done, 1)
                    dve.wait_ge(x1T_done, KC * g + u + 1)
                    dve.sem_inc(m_read, 1)
                elif step == "RT":
                    m = misc[:, 0:NT * 2 * E].rearrange("p (t n) -> p t n", t=NT)
                    dve.wait_ge(m_full, MISC[step, g, u] + 1)
                    then(nc.vector.tensor_copy(lg2[:, :, :], m[:, :, E:2 * E]))
                    nc.vector.tensor_tensor(lg[:, :, :], m[:, :, 0:E], lg2[:, :, :], ALU.add).then_inc(m_read, 1)
                    dve.wait_ge(m_read, MISC[step, g, u] + 1)
                    for t in range(NT):
                        last = nc.vector.max(top[:, t, :], lg[:, t, :])
                    then(last)
                    for t in range(NT):
                        last = nc.vector.max_index(topi[:, t, :], top[:, t, :], lg[:, t, :])
                    then(last)
                    then(nc.vector.tensor_copy(topf[:, :, :], topi[:, :, 0:2]))
                    nc.vector.tensor_tensor(gap[:, :], top[:, :, 0], top[:, :, 1], ALU.subtract).then_inc(gap_done, 1)
                    dve.wait_ge(th_done, g + 1)
                    nc.vector.tensor_scalar(wsel[:, :, 0], th[:, :], 0.5, 0.5, ALU.mult, ALU.add)
                    then(nc.vector.tensor_scalar(wsel[:, :, 1], th[:, :], -0.5, 0.5, ALU.mult, ALU.add))
                    if g == 0:
                        dve.wait_ge(consts, CONSTS_ALL)
                    for t in range(NT):
                        nc.vector.tensor_scalar(c1[:, t, :], iota_e[:, :], topf[:, t, 0:1], wsel[:, t, 0:1],
                                                ALU.is_equal, ALU.mult)
                        last = nc.vector.tensor_scalar(coef[:, t, :], iota_e[:, :], topf[:, t, 1:2], wsel[:, t, 1:2],
                                                       ALU.is_equal, ALU.mult)
                    then(last)
                    then(nc.vector.tensor_tensor(coef[:, :, :], coef[:, :, :], c1[:, :, :], ALU.add))
                    then(nc.vector.tensor_copy(coefhl[:, :, 0:E].bitcast(F32R), coef[:, :, :]))
                    nc.vector.tensor_tensor(coefhl[:, :, E:2 * E], coef[:, :, :], coefhl[:, :, 0:E],
                                            ALU.subtract).then_inc(coef_done, 1)
                elif step == "RC":
                    dve.wait_ge(m_full, MISC[step, g, u] + 1)
                    nc.vector.tensor_copy(coefT[:, g, :], misc[0:2 * E, :]).then_inc(coefT_done, 1)
                    dve.wait_ge(coefT_done, g + 1)
                    dve.sem_inc(m_read, 1)
                elif step == "GU":
                    n = FC * g + u
                    dve.wait_ge(silu_done, n + 1)
                    if n >= 3:
                        dve.wait_ge(hid, n - 2)
                    dve.wait_ge(up, n + 1)
                    nc.vector.tensor_tensor(gated[:, n % 3, :], up_bank(n)[:, :], silu_g[:, n % 2, :],
                                            ALU.mult).then_inc(gated_done, 1)
                elif step == "CB":
                    n = FC * g + u
                    dve.wait_ge(coefs, n + 1)
                    dve.wait_ge(gated_done, n + 1)
                    nc.vector.tensor_tensor(hidden[:, n % 2, :], coef_bank[:, :], gated[:, n % 3, :],
                                            ALU.mult).then_inc(hid, 1)
                elif step == "HL":
                    n = FC * g + u
                    dve.wait_ge(hid_hi, n + 1)
                    nc.vector.tensor_tensor(h_hl[:, n % 3, 1, :], hidden[:, n % 2, :], h_hl[:, n % 3, 0, :].bitcast(F32),
                                            ALU.subtract).then_inc(hid_lo, 1)

        @block.tensor
        def _(pe):
            def misc_free(step):
                if MISC[step] >= 1:
                    pe.wait_ge(m_read, MISC[step])

            pe.wait_ge(warm_set, 1)
            for _ in range(WARM):
                nc.tensor.matmul(s1_bank[0][:, :], warm[:, 0:P], warm[:, :], start=True, stop=True)

            for step, g, u in PLAN:
                if step in ("PROJ", "V"):
                    if g == 0 and (step == "PROJ" and u < 2 or step == "V" and u == 0):
                        pe.wait_ge(ld_w[1 - u % 2 if step == "PROJ" else 2], 16)
                    if step == "PROJ" and g == 1 and u == 0:
                        pe.wait_ge(ld_xT[KC], 16)
                    if (step, g, u) in EARLY:
                        n = EARLY[step, g, u]
                        dst = proj_bank[n % 3]
                        before = [s for s, m in EARLY.items() if m == n - 3]
                        if before and before[0][0] == "PROJ":
                            pe.wait_ge(qk_lo, 4 * before[0][1] + before[0][2] + 1)
                        elif before:
                            pe.wait_ge(v_done, 2 * before[0][1] + before[0][2] + 1)
                    else:
                        dst = misc
                        misc_free((step, g, u))
                    if step == "PROJ":
                        c = u // 2
                        for k in range(KC):
                            if g == 0 and u == 0:
                                pe.wait_ge(ld_xT[k], 16)
                            last = nc.tensor.matmul(dst[:, :], wqkv[:, 1 - u % 2, k, c * P:c * P + P],
                                                    xT[:, k, g * S:g * S + S], start=(k == 0), stop=(k == KC - 1))
                    else:
                        for m in range(2):
                            t = g * NT + 2 * u + m
                            for k in range(KC):
                                last = nc.tensor.matmul(dst[:, m * D:m * D + D], xT[:, k, t * P:t * P + P],
                                                        wqkv[:, 2, k, :], start=(k == 0), stop=(k == KC - 1))
                    last.then_inc(proj if (step, g, u) in EARLY else m_full, 1)
                elif step == "S1":
                    t, heads = UNITS1[u]
                    w = P * (t + 1)
                    n = NU * g + u
                    if u == 0:
                        pe.wait_ge(filled[g % SLOTS], 96 * (g // SLOTS + 1))
                    if n >= 3:
                        pe.wait_ge(s1_read, n - 2)
                    for m, h in enumerate(heads):
                        last = nc.tensor.matmul(s1_bank[n % 3][:, m * w:m * w + w],
                                                stacks[0:MAXROW, g % SLOTS, 1, h, t * P:t * P + P],
                                                stacks[0:MAXROW, g % SLOTS, 0, h, 0:w], start=True, stop=True)
                    last.then_inc(s1, 1)
                elif step == "NM":
                    pe.wait_ge(s1_read, NU * (g + 1))
                    if g == 0:
                        pe.wait_ge(consts, CONSTS)
                    else:
                        pe.wait_ge(nm_lo, g)
                    nc.tensor.transpose(nm_bank[0:QH * NT, 0:P], mx[:, g % 2].rearrange("p h t -> p (h t)"),
                                        ident[:, :]).then_inc(nm_t, 1)
                elif step == "S2":
                    j, heads = UNITS2[u]
                    w = S - P * j
                    n = NU * g + u
                    if n == 0:
                        pe.wait_ge(qk_lo, EARLY_QK)
                        pe.wait_ge(v_done, EARLY_V)
                    if u == 0:
                        pe.wait_ge(nm_in, 32 * (g + 1))
                    if n >= 2:
                        pe.wait_ge(exp_done, n - 1)
                    for m, h in enumerate(heads):
                        last = nc.tensor.matmul(s2_bank[n % 2][:, m * w:m * w + w],
                                                stacks[0:MAXROW + 2, g % SLOTS, 0, h, j * P:j * P + P],
                                                stacks[0:MAXROW + 2, g % SLOTS, 1, h, j * P:S], start=True, stop=True)
                    last.then_inc(s2, 1)
                elif step == "PV":
                    j = u
                    pe.wait_ge(masked, NT * g + j + 1)
                    if g >= 1 and j == 0:
                        pe.wait_ge(ot_copied, g)
                    for h in range(QH):
                        last = nc.tensor.matmul(pv_bank[32 * h:32 * h + VW, j * P:S],
                                                vv[:, g // NQ * NT + j, g % NQ * QH + h, :],
                                                pt[:, g % 2, h, SEG[j]:SEG[j] + S - P * j],
                                                start=(j == 0), stop=(j == NT - 1))
                    last.then_inc(pv, 1)
                elif step == "OT":
                    misc_free((step, g, u))
                    pe.wait_ge(ot_copied, g + 1)
                    for t in range(NT):
                        last = nc.tensor.transpose(misc[:, t * P:t * P + P], ot[:, g % 2, t * P:t * P + P], ident[:, :])
                    last.then_inc(m_full, 1)
                elif step == "OTR":
                    misc_free((step, g, u))
                    pe.wait_ge(attn_done, NQ * (g + 1))
                    for t in range(NT):
                        last = nc.tensor.transpose(misc[:, t * P:t * P + P], attn[:, t, u * P:u * P + P], ident[:, :])
                    last.then_inc(m_full, 1)
                elif step == "Y":
                    misc_free((step, g, u))
                    pe.wait_ge(ld_wp, 16)
                    for m in range(2):
                        t = 2 * u + m
                        for k in range(KC):
                            last = nc.tensor.matmul(misc[:, m * D:m * D + D], attnT[:, k, t * P:t * P + P], wp[:, k, :],
                                                    start=(k == 0), stop=(k == KC - 1))
                    last.then_inc(m_full, 1)
                elif step == "XT":
                    misc_free((step, g, u))
                    pe.wait_ge(ln_done, 2 * (g + 1))
                    for t in range(NT):
                        last = nc.tensor.transpose(misc[:, t * P:t * P + P], x[:, g * NT + t, u * P:u * P + P], ident[:, :])
                    last.then_inc(m_full, 1)
                elif step == "RL":
                    misc_free((step, g, u))
                    pe.wait_ge(x1T_done, KC * (g + 1))
                    pe.wait_ge(consts, CONSTS_ALL)
                    for k in range(KC):
                        for part in (1, 0):
                            last = nc.tensor.matmul(misc[0:2 * E, :], wr[:, k, :], x1T[:, part, g, k, :],
                                                    start=(k == 0 and part == 1), stop=(k == KC - 1 and part == 0))
                    last.then_inc(m_full, 1)
                elif step == "RT":
                    misc_free((step, g, u))
                    for t in range(NT):
                        last = nc.tensor.transpose(misc[:, t * 2 * E:t * 2 * E + 2 * E], lgT[:, t * P:t * P + P],
                                                   ident[0:2 * E, 0:2 * E])
                    last.then_inc(m_full, 1)
                elif step == "RC":
                    misc_free((step, g, u))
                    pe.wait_ge(coef_done, g + 1)
                    for t in range(NT):
                        last = nc.tensor.transpose(misc[0:2 * E, t * P:t * P + P], coefhl[:, t, :], ident[:, :])
                    last.then_inc(m_full, 1)
                elif step == "GU":
                    n = FC * g + u
                    if n == 0:
                        pe.wait_ge(gu_split, KC * 6)
                        pe.wait_ge(s1_read, NU * G)
                    if u == 0:
                        pe.wait_ge(x1T_done, KC * (g + 1))
                    for dst, col, done in ((gate_bank(n), u * P, gate), (up_bank(n), EI + u * P, up)):
                        if done is gate and n >= 2:
                            pe.wait_ge(gated_done, n - 1)
                        if done is up and n >= 1:
                            pe.wait_ge(silu_done, n)
                        for k in range(KC):
                            for w, part in ((gu_lo, 0), (gu_hi, 1), (gu_hi, 0)):
                                last = nc.tensor.matmul(dst[:, :], w[:, k, col:col + P], x1T[:, part, g, k, :],
                                                        start=(k == 0 and w is gu_lo), stop=(k == KC - 1 and w is gu_hi and part == 0))
                        last.then_inc(done, 1)
                elif step == "CB":
                    n = FC * g + u
                    if n == 0:
                        pe.wait_ge(nm_lo, G)
                    if u == 0:
                        pe.wait_ge(coefT_done, g + 1)
                    if n >= 1:
                        pe.wait_ge(hid, n)
                    nc.tensor.matmul(coef_bank[:, :], spread_r[:, u * P:u * P + P], coefT[:, g, :],
                                     start=True, stop=True).then_inc(coefs, 1)
                elif step == "DN":
                    n = FC * g + u
                    pe.wait_ge(hid_hi, n + 1)
                    pe.wait_ge(hid_lo, n + 1)
                    if n == 0:
                        pe.wait_ge(wd_split, FC)
                        pe.wait_ge(exp_done, NU * G)
                    if u == 0 and g >= 1:
                        pe.wait_ge(y_read, 2 * g)
                    for t in range(NT):
                        for part, w in ((1, 0), (0, 1), (0, 0)):
                            last = nc.tensor.matmul(y_bank[t // 2][:, t % 2 * D:t % 2 * D + D],
                                                    h_hl[:, n % 3, part, t * P:t * P + P], wd_hl[:, w, u, :],
                                                    start=(u == 0 and t % 2 == 0 and part == 1),
                                                    stop=(u == FC - 1 and part == 0 and w == 0), skip_group_check=True)
                        if t % 2:
                            last.then_inc(down, 1)


def kernel(L0_attn_x, L0_attn_Wq, L0_attn_Wk, L0_attn_Wv, L0_attn_Wp, L0_ffn_router_w, L0_ffn_gate_w, L0_ffn_up_w, L0_ffn_down_w):
    import numpy as np
    import concourse.bacc as bacc
    from concourse.bass_utils import run_bass_kernel_spmd

    def rows(a):
        return np.ascontiguousarray(a.reshape(-1, P, a.shape[1]).transpose(1, 0, 2))

    def by_group(w):
        return w.T.reshape(D, NQ, QH, HD).transpose(0, 1, 3, 2).reshape(D, D)

    x = np.asarray(L0_attn_x).reshape(B * S, D)
    wq, wk, wv, wp = (np.asarray(w) for w in (L0_attn_Wq, L0_attn_Wk, L0_attn_Wv, L0_attn_Wp))
    gate, up, down = (np.asarray(w) for w in (L0_ffn_gate_w, L0_ffn_up_w, L0_ffn_down_w))
    arrays = {
        "xT": rows(x.T), "x": rows(x),
        "wqkv": np.ascontiguousarray(np.stack([rows(by_group(wq)), rows(by_group(wk)), rows(wv.T)], axis=1)),
        "wp": rows(wp.T), "wr": rows(np.asarray(L0_ffn_router_w).T),
        "wgu": rows(np.concatenate([gate.reshape(EI, D).T, up.reshape(EI, D).T], axis=1)),
        "wd": rows(down.transpose(0, 2, 1).reshape(EI, D)),
    }
    nc = bacc.Bacc("TRN2", target_bir_lowering=False, num_devices=1)
    aps = [nc.dram_tensor(n + "_dram", a.shape, mybir.dt.from_np(a.dtype), kind="ExternalInput").ap() for n, a in arrays.items()]
    out = nc.dram_tensor("out_dram", [P, B * NT, D], F32, kind="ExternalOutput").ap()
    layer_kernel(nc, *aps, out)
    r = run_bass_kernel_spmd(nc, [{n + "_dram": a for n, a in arrays.items()}], core_ids=[0])
    return np.ascontiguousarray(r.results[0]["out_dram"].transpose(1, 0, 2)).reshape(B, S, D)
```

```python
from contextlib import ExitStack

import concourse.bass as bass
from concourse import mybir

F32 = mybir.dt.float32
F32R = mybir.dt.float32r
BF16 = mybir.dt.bfloat16
U32 = mybir.dt.uint32
ALU = mybir.AluOpType
ACT = mybir.ActivationFunctionType
AX = mybir.AxisListType

P = 128
B, S, D = 2, 512, 256
H, HD = 16, 16
KC = D // P
NT = S // P
QH = 4
NQ = H // QH
G = B * NQ
E, I = 8, 96
EI = E * I
FC = EI // P
EPS = 1e-5
SCALE = HD ** -0.5
MASKED = -1e30

PARTS = ((0, 1, 0), (2, 2, 3))
MAXROW = 96
SLOT = [0, 1, 2, 3, 0, 1, 2, 0]
SLOTS = 4
FILLS = [SLOT[:g + 1].count(SLOT[g]) for g in range(G)]
SEG = [0, 512, 896, 1152]
PTW = 1280
VW = 32

UNITS1 = [(3, [h]) for h in range(4)] + [(2, [h]) for h in range(4)] + [(1, [0, 1]), (1, [2, 3]), (0, [0, 1, 2, 3])]
UNITS2 = [(3 - t, hs) for t, hs in UNITS1]
NU = len(UNITS1)
MASK_MADE = 2
IDENT_MADE = 4
SLOT_MADE = [0, 5, 6, 7]
CONSTS = 9
CONSTS_ALL = CONSTS + E + 8
WARM = 7
MASK_AFTER = [4, 8, 10, 11]
PIECES = KC * 2 * EI // D
PV_UNITS = [2, 4, 6, 8]
LEAD = NU + 8


def chain(b):
    return [("OTR", b, 0), ("OTR", b, 1), ("Y", b, 0), ("Y", b, 1), ("RS", b, 0), ("LN1", b, 0), ("XT", b, 0), ("XT", b, 1),
            ("RL", b, 0), ("RT", b, 0), ("RW", b, 0), ("RC", b, 0)]


def make_plan():
    plan = [(step, 0, n) for n in range(4) for step in ("PROJ", "PL")] + [("V", 0, 0)]
    projections = {2: ("V", 0, 1), 5: ("PROJ", 1, 0), 6: ("PL", 1, 0), 9: ("PROJ", 1, 1), 11: ("PL", 1, 1),
                   14: ("PROJ", 1, 2), 16: ("PL", 1, 2), LEAD + 2: ("PROJ", 1, 3), LEAD + 3: ("PL", 1, 3),
                   LEAD + 9: ("V", 1, 0), LEAD + 20: ("V", 1, 1)}
    links = dict(zip([(5, 2), (5, 4), (5, 6), (5, 7), (5, 8), (6, 0), (6, 3), (6, 6), (6, 9), (7, 0), (7, 1), (7, 4)], chain(0)))
    split_from, first_expert = (5, 5), (7, 2)
    for s in range(G * NU + LEAD):
        if s < G * NU:
            plan.append(("S1", s // NU, s % NU))
        if s in projections:
            plan.append(projections[s])
        if NU < s < (G + 1) * NU and s % NU in (2, 3):
            plan.append(("NM" if s % NU == 2 else "NL", s // NU - 1, 0))
        if s >= LEAD:
            g, u = divmod(s - LEAD, NU)
            plan.append(("S2", g, u))
            if g >= 1 and u in PV_UNITS:
                plan.append(("PV", g - 1, PV_UNITS.index(u)))
            if g >= 1 and u == 8:
                plan.append(("OC", g - 1, 0))
            if g >= 2 and u == 0:
                plan.append(("OT", g - 2, 0))
            if (g, u) in links:
                plan.append(links[g, u])
            if (g, u) == first_expert:
                plan.append(("GU", 0, 0))
            if g in (3, 4, 5) and u in (1, 3, 5, 7):
                plan.append(("GH", 0, 4 * (g - 3) + u // 2))
            if 0 <= s - LEAD - NU * split_from[0] - split_from[1] < PIECES:
                plan.append(("GL", 0, s - LEAD - NU * split_from[0] - split_from[1]))
            if g == 6 and u < FC:
                plan.append(("WH", 0, u))
    plan += [("SG", 0, 0), ("GT", 0, 0), ("PV", G - 1, 0), ("PV", G - 1, 1), ("OT", G - 2, 0)]
    plan += [("PV", G - 1, 2), ("PV", G - 1, 3), ("OC", G - 1, 0)] + [("WL", 0, c) for c in range(FC)]
    plan += [("GU", 0, 1), ("SG", 0, 1), ("GT", 0, 1), ("CB", 0, 0), ("OT", G - 1, 0), ("HL", 0, 0)]
    plan += [("GU", 0, 2), ("SG", 0, 2), ("GT", 0, 2)]
    links = chain(1)
    for n, line in enumerate(["L L GU SG CB1 L GT HL1 L DN0",
                              "GU SG L L CB2 GT HL2 DN1",
                              "L L GU SG CB3 GT HL3 DN2",
                              "L GU SG CB4 L GT HL4 DN3",
                              "L GU SG CB5 GT HL5 DN4",
                              "GU SG L DN5 CB6 GT HL6 YS",
                              "GU SG CB7 GT HL7 DN6 LN",
                              "GU SG CB8 GT HL8 DN7",
                              "CB9 HL9 GU SG DN8 CB10 GT HL10 DN9",
                              "CB11 HL11 DN10 YR DN11 YS LN"], 3):
        for word in line.split():
            m = (int(word[2:] or n) // FC, int(word[2:] or n) % FC) if word != "L" else None
            batch = 0 if n < B * FC - 2 else 1
            step = {"L": "", "LN": "LN2"}.get(word[0:2], word[0:2])
            plan += links[0:1] if not step else [(step, batch, 0)] if step in ("YS", "YR", "LN2") else [(step, *m)]
            if word == "L":
                links.pop(0)
    assert not links
    return plan


PLAN = make_plan()
EARLY = {s: n for n, s in enumerate([s for s in PLAN[:PLAN.index(("S2", 0, 0))] if s[0] in ("PROJ", "V")])}
LATE = [s for s in PLAN if s[0] in ("PROJ", "V") and s not in EARLY]
EARLY_QK = sum(s[0] == "PROJ" for s in EARLY)
EARLY_V = len(EARLY) - EARLY_QK
MISC = {s: n for n, s in enumerate([s for s in PLAN if s in LATE or s[0] in ("NM", "OT", "OTR", "Y", "XT", "RL", "RT", "RC")])}


def layer_kernel(nc, xT_d, x_d, wqkv_d, wp_d, wr_d, wgu_d, wd_d, out_d):
    with ExitStack() as ctx:
        def sb(name, shape, dt=F32):
            return ctx.enter_context(nc.sbuf_tensor(name, shape, dt))

        def sem(name):
            return ctx.enter_context(nc.semaphore(name))

        early = sb("early", [P, 14 * 256])
        xT = early[:, 0:KC * B * S].rearrange("p (k n) -> p k n", k=KC)
        wqkv = early[:, KC * B * S:].rearrange("p (w k n) -> p w k n", w=3, k=KC)
        gu_raw = early[:, 0:KC * 2 * EI].rearrange("p (k n) -> p k n", k=KC)
        wp = sb("wp", [P, KC, D])
        wd_raw = sb("wd_raw", [P, FC, D])
        wr_raw = sb("wr_raw", [P, KC, E])
        wr = sb("wr", [P, KC, 2 * E], F32R)
        x = sb("x", [P, B * NT, D])
        qk = [sb(f"qk{b}", [P, 4, KC, S], F32R) for b in range(B)]
        gu_hi = qk[0][:, 0:3].rearrange("p a k n -> p (a k n)").rearrange("p (k n) -> p k n", k=KC)
        gu_lo = qk[1][:, 0:3].rearrange("p a k n -> p (a k n)").rearrange("p (k n) -> p k n", k=KC)
        vv = sb("vv", [P, B * NT, H, VW])
        own_slots = sb("own_slots", [P, SLOTS - 1, 2, QH, S], F32R)
        x1T = sb("x1T", [P, 2, B, KC, S], F32R)
        stack = [own_slots[:, n] for n in range(SLOTS - 1)]
        stack.append(x1T[:, :].rearrange("p a b k n -> p (a b k n)").rearrange("p (a h n) -> p a h n", a=2, h=QH))
        flat = [v.rearrange("p a h n -> p (a h n)") for v in stack[:-1]]
        h_hl = flat[2][:, 0:3 * 2 * S].rearrange("p (r a n) -> p r a n", r=3, a=2)
        wd_hl = flat[1][:, 0:2 * FC * D].rearrange("p (a c n) -> p a c n", a=2, c=FC)
        pt = sb("pt", [P, 2, QH, PTW])
        warm = pt[:, 1, 0, 0:S // 2].bitcast(BF16)
        temps = early
        silu_g = temps[:, 0:2 * S].rearrange("p (r n) -> p r n", r=2)
        gated = temps[:, 2 * S:5 * S].rearrange("p (r n) -> p r n", r=3)
        hidden = temps[:, 5 * S:7 * S].rearrange("p (r n) -> p r n", r=2)
        ot = sb("ot", [P, 2, S])
        attn = sb("attn", [P, NT, D])
        attnT = sb("attnT", [P, KC, S])
        mx = sb("mx", [P, 2, QH, NT])
        nm = [sb("nm_hi", [QH * NT, P], F32R), sb("nm_lo", [QH * NT, P], F32R)]
        rden = sb("rden", [P, 2, NT, QH])
        stats = sb("stats", [P, 2 * B * NT, 6])
        mv = sb("mv", [P, 2 * B * NT, 2])
        var_eps = sb("var_eps", [P, 2 * B * NT])
        rstd = sb("rstd", [P, 2 * B * NT])
        lgT = sb("lgT", [2 * E, S])
        lg2 = sb("lg2", [P, NT, E])
        lg = sb("lg", [P, NT, E])
        top = sb("top", [P, NT, E])
        topi = sb("topi", [P, NT, E], U32)
        topf = sb("topf", [P, NT, 2])
        is_best = sb("is_best", [P, 2, NT, E])
        gap = sb("gap", [P, NT])
        th = sb("th", [P, NT])
        wsel = sb("wsel", [P, NT, 2])
        c1 = sb("c1", [P, NT, E])
        coef = sb("coef", [P, NT, E])
        coefhl = sb("coefhl", [P, NT, 2 * E])
        coefT = qk[0][0:2 * E, 3, :, :]
        ident = sb("ident", [P, P])
        ident_r = sb("ident_r", [P, P], F32R)
        mask = sb("mask", [P, S], BF16)
        spread = attnT[0:2 * E].rearrange("p k n -> p (k n)")[:, 0:EI]
        spread_r = sb("spread_r", [2 * E, EI], F32R)
        iota_e = sb("iota_e", [P, E])
        minus_half = sb("minus_half", [P, NT])

        bank = [ctx.enter_context(nc.psum_tensor(f"bank{n}", [P, 512], F32)) for n in range(8)]
        s1_bank, s2_bank, pv_bank = bank[0:3], [bank[3], bank[4], bank[6]], bank[5]
        proj_bank = bank[3:6]
        ffn_bank, coef_bank, y_bank = bank[0:3], bank[6], [bank[3:5], [bank[5], bank[7]]]

        def misc_bank(step):
            return bank[5] if step in chain(1) and (MISC[step] - MISC["OTR", 1, 0]) % 2 else bank[7]

        def gate_bank(n):
            return ffn_bank[2 * n % 3]

        def up_bank(n):
            return ffn_bank[(2 * n + 1) % 3]

        ld_xT = [sem(n) for n in ("ld_xT0_k0", "ld_xT0_k1", "ld_xT1")]
        ld_wp, ld_x, ld_wr, ld_gu, ld_wd = (sem(n) for n in ("ld_wp", "ld_x", "ld_wr", "ld_gu", "ld_wd"))
        ld_w = [sem(f"ld_w{n}") for n in "qkv"]
        consts = sem("consts")
        pool_own = sem("pool_own")
        proj = sem("proj")
        qk_hi = sem("qk_hi")
        qk_lo = sem("qk_lo")
        v_done = sem("v_done")
        warm_set = sem("warm_set")
        slot0_set = sem("slot0_set")
        ones_in = sem("ones_in")
        filled = [sem(f"filled{n}") for n in range(SLOTS)]
        s1 = sem("s1")
        s1_read = sem("s1_read")
        nm_hi = sem("nm_hi_done")
        nm_lo = sem("nm_lo_done")
        nm_in = [sem("nm_in_hi"), sem("nm_in_lo")]
        s2 = sem("s2")
        exp_done = sem("exp_done")
        masked = sem("masked")
        pv = sem("pv")
        ot_copied = sem("ot_copied")
        m_full = sem("m_full")
        m_read = sem("m_read")
        dve_own = sem("dve_own")
        attn_done = sem("attn_done")
        stat_done = sem("stat_done")
        rstd_done = sem("rstd_done")
        ln_done = sem("ln_done")
        x1T_hi = sem("x1T_hi")
        x1T_done = sem("x1T_done")
        gap_done = sem("gap_done")
        th_done = sem("th_done")
        coef_done = sem("coef_done")
        coefT_done = sem("coefT_done")
        gu_hi_done = sem("gu_hi_done")
        gu_split = sem("gu_split")
        wd_hi_done = sem("wd_hi_done")
        wd_split = sem("wd_split")
        gate = sem("gate")
        up = sem("up")
        coefs = sem("coefs")
        silu_done = sem("silu_done")
        gated_done = sem("gated_done")
        hid = sem("hid")
        hid_hi = sem("hid_hi")
        hid_lo = sem("hid_lo")
        down = sem("down")
        stored = sem("stored")

        def projected(eng, step):
            if step in EARLY:
                eng.wait_ge(proj, EARLY[step] + 1)
                return proj_bank[EARLY[step] % 3]
            eng.wait_ge(m_full, MISC[step] + 1)
            return misc_bank(step)

        block = ctx.enter_context(nc.Block())

        @block.sync
        def _(sp):
            for k in range(KC):
                sp.dma_start(xT[:, k, 0:S], xT_d[:, k, 0:S]).then_inc(ld_xT[k], 16)
            sp.dma_start(wqkv[:, 2], wqkv_d[:, 2]).then_inc(ld_w[2], 16)
            sp.dma_start(xT[:, :, S:2 * S], xT_d[:, :, S:2 * S]).then_inc(ld_xT[KC], 16)

            def fill(g):
                b, c, r = g // NQ, g % NQ // 2, 64 * (g % 2)
                if FILLS[g] > 1:
                    sp.wait_ge(s2, NU * (max(n for n in range(g) if SLOT[n] == SLOT[g]) + 1))
                elif g == 0:
                    sp.wait_ge(slot0_set, 3)
                else:
                    sp.wait_ge(consts, SLOT_MADE[g])
                for part in range(4):
                    sp.wait_ge(qk_lo if part % 2 else qk_hi, 4 * b + 2 * c + part // 2 + 1)
                    for n in range(3):
                        if PARTS[part // 2][n] == part:
                            sp.dma_start(stack[SLOT[g]][HD * n:HD * n + HD, part // 2, :, :].bitcast(F32),
                                         qk[b][r:r + 64, part, c, :].bitcast(F32)).then_inc(filled[SLOT[g]], 16)

            sp.dma_start(wr_raw[:, :, :], wr_d).then_inc(ld_wr, 16)
            fill(0)
            fill(1)
            for n in range(1, SLOTS):
                sp.dma_start(stack[n][MAXROW:MAXROW + 2, 0].bitcast(F32),
                             stack[0][MAXROW:MAXROW + 2, 0].bitcast(F32)).then_inc(ones_in, 16)
            fill(2)
            for step, g, u in PLAN:
                if step in ("NM", "NL"):
                    n = 0 if step == "NM" else 1
                    sp.wait_ge((nm_hi, nm_lo)[n], g + 1)
                    sp.dma_start(stack[SLOT[g]][MAXROW + n:MAXROW + n + 1, 1, :, :].bitcast(F32),
                                 nm[n][:, :].bitcast(F32)).then_inc(nm_in[n], 16)
                    if step == "NL" and g == 0:
                        fill(3)
                        sp.dma_start(x[:, :, :], x_d).then_inc(ld_x, 16)
                        sp.dma_start(wp[:, :, :], wp_d).then_inc(ld_wp, 16)
                        sp.dma_start(wd_raw[:, :, :], wd_d).then_inc(ld_wd, 16)
                    if step == "NL" and g == 2:
                        sp.wait_ge(m_full, MISC[LATE[-1]] + 1)
                        sp.dma_start(gu_raw, wgu_d).then_inc(ld_gu, 16)
                if step == "S2" and u == NU - 1:
                    for n in [n for n in range(g + 1, G) if SLOT[n] == SLOT[g]][0:1]:
                        fill(n)
                if step == "LN2":
                    for t in range(g * NT, g * NT + NT, 2):
                        sp.wait_ge(ln_done, (B * NT + t) // 2 + 1)
                        sp.dma_start(out_d[:, t:t + 2, :], x[:, t:t + 2, :]).then_inc(stored, 16)
            sp.wait_ge(stored, 16 * B * NT // 2)

        @block.gpsimd
        def _(pool):
            made = 0

            def make(ins):
                nonlocal made
                made += 1
                ins.then_inc(consts, 1)
                pool.wait_ge(consts, made)

            make(nc.gpsimd.memset(mask[:, :], 0.0))
            make(nc.gpsimd.affine_select(out=mask[:, S - P:S], in_=mask[:, S - P:S], compare_op=ALU.is_ge, fill=MASKED, base=0,
                                         pattern=[[-1, P]], channel_multiplier=1))
            assert made == MASK_MADE
            make(nc.gpsimd.memset(ident[:, :], 0.0))
            make(nc.gpsimd.affine_select(out=ident[:, :], in_=ident[:, :], compare_op=ALU.not_equal, fill=1.0, base=0,
                                         pattern=[[-1, P]], channel_multiplier=1))
            assert made == IDENT_MADE
            for n in range(1, SLOTS):
                make(nc.gpsimd.memset(stack[n][0:MAXROW].bitcast(F32), 0.0))
                assert made == SLOT_MADE[n]
            make(nc.gpsimd.memset(vv[:, :, :, HD:HD + 1], 1.0))
            make(nc.gpsimd.memset(vv[:, :, :, HD + 1:VW], 0.0))
            assert made == CONSTS
            make(nc.gpsimd.memset(minus_half[:, :], -0.5))
            for e in range(E):
                make(nc.gpsimd.memset(iota_e[:, e:e + 1], float(e)))
            make(nc.gpsimd.memset(spread[:, :], 0.0))
            for n in range(2):
                v = spread[:, :].rearrange("p (e i) -> p e i", e=E)
                make(nc.gpsimd.affine_select(out=v, in_=v, compare_op=ALU.not_equal, fill=1.0, base=-E * n,
                                             pattern=[[-1, E], [0, I]], channel_multiplier=1))
            make(nc.gpsimd.tensor_copy(spread_r[:, :], spread[:, :]))
            make(nc.gpsimd.tensor_copy(ident_r[:, :], ident[:, :]))
            pool.wait_ge(ld_wr, 16)
            make(nc.gpsimd.tensor_copy(wr[:, :, 0:E], wr_raw[:, :, :]))
            make(nc.gpsimd.tensor_tensor(wr[:, :, E:2 * E], wr_raw[:, :, :], wr[:, :, 0:E].bitcast(F32), ALU.subtract))
            assert made == CONSTS_ALL
            own = 0

            def then(ins):
                nonlocal own
                own += 1
                ins.then_inc(pool_own, 1)
                pool.wait_ge(pool_own, own)


            for step, g, u in PLAN:
                if step == "S2" and u + 1 in MASK_AFTER:
                    j = MASK_AFTER.index(u + 1)
                    pool.wait_ge(exp_done, NU * g + u + 1)
                    v = pt[:, g % 2, :, SEG[j]:SEG[j] + P]
                    nc.gpsimd.affine_select(out=v, in_=v, compare_op=ALU.is_ge, fill=0.0, base=0,
                                            pattern=[[0, QH], [1, P]], channel_multiplier=-1).then_inc(masked, 1)
                if step == "GL":
                    if u == 0:
                        for n in range(SLOTS):
                            pool.wait_ge(filled[n], 96 * SLOT.count(n))
                    k, cols = u // 6, slice(u % 6 * D, u % 6 * D + D)
                    pool.wait_ge(gu_hi_done, u + 1)
                    nc.gpsimd.tensor_tensor(gu_lo[:, k, cols], gu_raw[:, k, cols], gu_hi[:, k, cols].bitcast(F32),
                                            ALU.subtract).then_inc(gu_split, 1)
                if step == "WL":
                    pool.wait_ge(wd_hi_done, u + 1)
                    nc.gpsimd.tensor_tensor(wd_hl[:, 1, u, :], wd_raw[:, u, :], wd_hl[:, 0, u, :].bitcast(F32),
                                            ALU.subtract).then_inc(wd_split, 1)
                if step == "RS" or step == "YS":
                    first = NT * g if step == "RS" else NT * (B + g)
                    step_n = NT if step == "RS" else 2
                    for n in range(first, first + NT, step_n):
                        m = n + step_n
                        pool.wait_ge(stat_done, m)
                        then(nc.gpsimd.tensor_scalar(var_eps[:, n:m], mv[:, n:m, 1], EPS, None, ALU.add))
                        nc.gpsimd.tensor_tensor(rstd[:, n:m], var_eps[:, n:m], minus_half[:, 0:step_n],
                                                ALU.pow).then_inc(rstd_done, step_n // 2)

        @block.scalar
        def _(act):
            act.dma_start(wqkv[:, 1], wqkv_d[:, 1]).then_inc(ld_w[1], 16)
            act.dma_start(wqkv[:, 0], wqkv_d[:, 0]).then_inc(ld_w[0], 16)
            for step, g, u in PLAN:
                misc = misc_bank((step, g, u)) if (step, g, u) in MISC else None
                if step == "PROJ":
                    src = projected(act, (step, g, u))
                    nc.scalar.copy(qk[g][:, 2 * (u % 2), u // 2, :], src[:, :]).then_inc(qk_hi, 1)
                elif step == "V":
                    src = projected(act, (step, g, u))
                    t = g * NT + 2 * u
                    nc.scalar.copy(vv[:, t:t + 2, :, 0:HD],
                                   src[:, :].rearrange("p (t h d) -> p t h d", t=2, h=H)).then_inc(v_done, 1)
                    if (step, g, u) in LATE:
                        act.wait_ge(v_done, 2 * g + u + 1)
                        act.sem_inc(m_read, 1)
                elif step == "GH":
                    if u == 0:
                        act.wait_ge(ld_gu, 16)
                        for n in range(SLOTS):
                            act.wait_ge(filled[n], 96 * SLOT[:NQ].count(n))
                    k, cols = u // 6, slice(u % 6 * D, u % 6 * D + D)
                    nc.scalar.copy(gu_hi[:, k, cols], gu_raw[:, k, cols]).then_inc(gu_hi_done, 1)
                elif step == "WH":
                    if u == 0:
                        act.wait_ge(ld_wd, 16)
                        act.wait_ge(s2, NU * 6)
                    nc.scalar.copy(wd_hl[:, 0, u, :], wd_raw[:, u, :]).then_inc(wd_hi_done, 1)
                elif step == "NM":
                    act.wait_ge(m_full, MISC[step, g, u] + 1)
                    if g >= 1:
                        act.wait_ge(nm_in[0], 16 * g)
                        act.wait_ge(nm_lo, g)
                    nc.scalar.mul(nm[0][:, :], misc[0:QH * NT, 0:P], -1.0).then_inc(nm_hi, 1)
                elif step == "S2":
                    j, heads = UNITS2[u]
                    w = S - P * j
                    n = NU * g + u
                    act.wait_ge(s2, n + 1)
                    if g >= 2 and u == 0:
                        act.wait_ge(pv, NT * (g - 1))
                    nc.scalar.activation(pt[:, g % 2, heads[0]:heads[-1] + 1, SEG[j]:SEG[j] + w],
                                         s2_bank[n % 3][:, 0:w * len(heads)].rearrange("p (h n) -> p h n", h=len(heads)),
                                         ACT.Exp, scale=SCALE).then_inc(exp_done, 1)
                elif step == "OC":
                    act.wait_ge(pv, NT * (g + 1))
                    if g >= 2:
                        act.wait_ge(m_full, MISC["OT", g - 2, 0] + 1)
                    nc.scalar.copy(ot[:, g % 2, :], pv_bank[:, :]).then_inc(ot_copied, 1)
                elif step == "OTR":
                    act.wait_ge(m_full, MISC[step, g, u] + 1)
                    if g == 0 and u == 0:
                        act.wait_ge(consts, CONSTS_ALL)
                    nc.scalar.copy(attnT[:, u, :], misc[:, :]).then_inc(m_read, 1)
                elif step == "XT":
                    act.wait_ge(m_full, MISC[step, g, u] + 1)
                    nc.scalar.copy(x1T[:, 0, g, u, :], misc[:, :]).then_inc(x1T_hi, 1)
                elif step == "RL":
                    act.wait_ge(m_full, MISC[step, g, u] + 1)
                    nc.scalar.copy(lgT[:, :], misc[0:2 * E, :]).then_inc(m_read, 1)
                elif step == "RW":
                    act.wait_ge(gap_done, g + 1)
                    nc.scalar.activation(th[:, :], gap[:, :], ACT.Tanh, scale=0.5).then_inc(th_done, 1)
                elif step == "SG":
                    n = FC * g + u
                    act.wait_ge(gate, n + 1)
                    if n == 0:
                        act.wait_ge(gu_split, PIECES)
                    if n >= 2:
                        act.wait_ge(gated_done, n - 1)
                    nc.scalar.activation(silu_g[:, n % 2, :], gate_bank(n)[:, :], ACT.Silu).then_inc(silu_done, 1)
                elif step == "CB":
                    n = FC * g + u
                    act.wait_ge(hid, n + 1)
                    if n >= 3:
                        act.wait_ge(down, 2 * (n - 2))
                    nc.scalar.copy(h_hl[:, n % 3, 0, :], hidden[:, n % 2, :]).then_inc(hid_hi, 1)

        @block.vector
        def _(dve):
            own = 0

            def then(ins):
                nonlocal own
                own += 1
                ins.then_inc(dve_own, 1)
                dve.wait_ge(dve_own, own)

            def norm_stats(n, src):
                for i in range(n, n + 2):
                    last = nc.vector.bn_stats(stats[:, i, :], src[i - n])
                then(last)
                for i in range(n, n + 2):
                    last = nc.vector.bn_aggr(mv[:, i, :], stats[:, i, :])
                last.then_inc(stat_done, 2)

            def norm_apply(n, src):
                dve.wait_ge(rstd_done, n // 2 + 1)
                for i in range(n, n + 2):
                    last = nc.vector.tensor_scalar(x[:, i % (B * NT), :], src[i - n], mv[:, i, 0:1], rstd[:, i:i + 1],
                                                   ALU.subtract, ALU.mult)
                last.then_inc(ln_done, 1)

            def y_tiles(g, m):
                t = g * NT + 2 * m
                return [x[:, t, :], x[:, t + 1, :]] if g < B - 1 else [y_bank[g][m][:, 0:D], y_bank[g][m][:, D:2 * D]]

            nc.vector.memset(warm[:, :], 0.0).then_inc(warm_set, 1)
            for side in range(2):
                nc.vector.memset(stack[0][0:MAXROW, side].bitcast(F32), 0.0).then_inc(slot0_set, 1)
            nc.vector.memset(stack[0][MAXROW:MAXROW + 2, 0].bitcast(F32), 1.0).then_inc(slot0_set, 1)
            for step, g, u in PLAN:
                misc = misc_bank((step, g, u)) if (step, g, u) in MISC else None
                if step == "PL":
                    side = 2 * (u % 2)
                    src = projected(dve, ("PROJ", g, u))
                    dve.wait_ge(qk_hi, 4 * g + u + 1)
                    nc.vector.tensor_tensor(qk[g][:, side + 1, u // 2, :], src[:, :],
                                            qk[g][:, side, u // 2, :].bitcast(F32), ALU.subtract).then_inc(qk_lo, 1)
                    if ("PROJ", g, u) in LATE:
                        dve.wait_ge(qk_lo, 4 * g + u + 1)
                        dve.sem_inc(m_read, 1)
                elif step == "S1":
                    t, heads = UNITS1[u]
                    w = P * (t + 1)
                    n = NU * g + u
                    dve.wait_ge(s1, n + 1)
                    if n == 0:
                        dve.wait_ge(consts, MASK_MADE)
                    for m, h in enumerate(heads):
                        scores = s1_bank[n % 3][:, m * w:m * w + w]
                        last = nc.vector.tensor_tensor_reduce(scores, scores, mask[:, S - w:S], 1.0, MASKED, ALU.add,
                                                              ALU.max, mx[:, g % 2, h, t:t + 1])
                    last.then_inc(s1_read, 1)
                elif step == "NL":
                    misc = misc_bank(("NM", g, u))
                    dve.wait_ge(nm_hi, g + 1)
                    if g >= 1:
                        dve.wait_ge(nm_in[1], 16 * g)
                    nc.vector.scalar_tensor_tensor(out=nm[1][:, :], in0=misc[0:QH * NT, 0:P], scalar=-1.0,
                                                   in1=nm[0][:, :].bitcast(F32), op0=ALU.mult,
                                                   op1=ALU.subtract).then_inc(nm_lo, 1)
                    dve.wait_ge(nm_lo, g + 1)
                    dve.sem_inc(m_read, 1)
                elif step == "OT":
                    m = misc[:, :].rearrange("p (t h c) -> p t h c", t=NT, h=QH)
                    dve.wait_ge(m_full, MISC[step, g, u] + 1)
                    if g == NQ:
                        dve.wait_ge(m_full, MISC["OTR", 0, 1] + 1)
                    then(nc.vector.reciprocal(rden[:, g % 2], m[:, :, :, HD]))
                    q = g % NQ
                    o = attn[:, :, q * 64:q * 64 + 64].rearrange("p t (h d) -> p t h d", h=QH)
                    nc.vector.tensor_tensor(o, m[:, :, :, 0:HD], rden[:, g % 2].unsqueeze(3).to_broadcast([P, NT, QH, HD]),
                                            ALU.mult).then_inc(attn_done, 1)
                    dve.wait_ge(attn_done, g + 1)
                    dve.sem_inc(m_read, 1)
                elif step == "Y":
                    dve.wait_ge(m_full, MISC[step, g, u] + 1)
                    if g == 0 and u == 0:
                        dve.wait_ge(ld_x, 16)
                    t = g * NT + 2 * u
                    own_x = x[:, t:t + 2, :].rearrange("p t n -> p (t n)")
                    nc.vector.tensor_tensor(own_x, misc[:, :], own_x, ALU.add).then_inc(m_read, 1)
                    dve.wait_ge(m_read, MISC[step, g, u] + 1)
                    norm_stats(t, [x[:, t, :], x[:, t + 1, :]])
                elif step == "LN1":
                    for n in range(NT * g, NT * g + NT, 2):
                        norm_apply(n, [x[:, n, :], x[:, n + 1, :]])
                elif step == "YS":
                    for m in range(2):
                        dve.wait_ge(down, 2 * (FC * g + FC - 1) + m + 1)
                        if g < B - 1:
                            t = g * NT + 2 * m
                            own_x = x[:, t:t + 2, :].rearrange("p t n -> p (t n)")
                            then(nc.vector.tensor_tensor(own_x, y_bank[g][m][:, :], own_x, ALU.add))
                        norm_stats(NT * (B + g) + 2 * m, y_tiles(g, m))
                elif step == "LN2":
                    for m in range(2):
                        norm_apply(NT * (B + g) + 2 * m, y_tiles(g, m))
                elif step == "XT":
                    dve.wait_ge(x1T_hi, KC * g + u + 1)
                    nc.vector.tensor_tensor(x1T[:, 1, g, u, :], misc[:, :], x1T[:, 0, g, u, :].bitcast(F32),
                                            ALU.subtract).then_inc(x1T_done, 1)
                    dve.wait_ge(x1T_done, KC * g + u + 1)
                    dve.sem_inc(m_read, 1)
                elif step == "RT":
                    m = misc[:, 0:NT * 2 * E].rearrange("p (t n) -> p t n", t=NT)
                    dve.wait_ge(m_full, MISC[step, g, u] + 1)
                    then(nc.vector.tensor_copy(lg2[:, :, :], m[:, :, E:2 * E]))
                    nc.vector.tensor_tensor(lg[:, :, :], m[:, :, 0:E], lg2[:, :, :], ALU.add).then_inc(m_read, 1)
                    dve.wait_ge(m_read, MISC[step, g, u] + 1)
                    for t in range(NT):
                        last = nc.vector.max(top[:, t, :], lg[:, t, :])
                    then(last)
                    for t in range(NT):
                        last = nc.vector.max_index(topi[:, t, :], top[:, t, :], lg[:, t, :])
                    then(last)
                    then(nc.vector.tensor_copy(topf[:, :, :], topi[:, :, 0:2]))
                    nc.vector.tensor_tensor(gap[:, :], top[:, :, 0], top[:, :, 1], ALU.subtract).then_inc(gap_done, 1)
                    if g == 0:
                        dve.wait_ge(consts, CONSTS_ALL)
                    for n in range(2):
                        last = nc.vector.tensor_tensor(is_best[:, n], iota_e[:, :].unsqueeze(1).to_broadcast([P, NT, E]),
                                                       topf[:, :, n:n + 1].to_broadcast([P, NT, E]), ALU.is_equal)
                    then(last)
                elif step == "RW":
                    dve.wait_ge(th_done, g + 1)
                    nc.vector.tensor_scalar(wsel[:, :, 0], th[:, :], 0.5, 0.5, ALU.mult, ALU.add)
                    then(nc.vector.tensor_scalar(wsel[:, :, 1], th[:, :], -0.5, 0.5, ALU.mult, ALU.add))
                    for n, c in ((0, c1), (1, coef)):
                        last = nc.vector.tensor_tensor(c[:, :, :], is_best[:, n], wsel[:, :, n:n + 1].to_broadcast([P, NT, E]),
                                                       ALU.mult)
                    then(last)
                    then(nc.vector.tensor_tensor(coef[:, :, :], coef[:, :, :], c1[:, :, :], ALU.add))
                    then(nc.vector.tensor_copy(coefhl[:, :, 0:E].bitcast(F32R), coef[:, :, :]))
                    nc.vector.tensor_tensor(coefhl[:, :, E:2 * E], coef[:, :, :], coefhl[:, :, 0:E],
                                            ALU.subtract).then_inc(coef_done, 1)
                elif step == "RC":
                    dve.wait_ge(m_full, MISC[step, g, u] + 1)
                    nc.vector.tensor_copy(coefT[:, g, :], misc[0:2 * E, :]).then_inc(coefT_done, 1)
                    dve.wait_ge(coefT_done, g + 1)
                    dve.sem_inc(m_read, 1)
                elif step == "GT":
                    n = FC * g + u
                    dve.wait_ge(silu_done, n + 1)
                    if n >= 3:
                        dve.wait_ge(hid, n - 2)
                    dve.wait_ge(up, n + 1)
                    nc.vector.tensor_tensor(gated[:, n % 3, :], up_bank(n)[:, :], silu_g[:, n % 2, :],
                                            ALU.mult).then_inc(gated_done, 1)
                elif step == "CB":
                    n = FC * g + u
                    dve.wait_ge(coefs, n + 1)
                    dve.wait_ge(gated_done, n + 1)
                    nc.vector.tensor_tensor(hidden[:, n % 2, :], coef_bank[:, :], gated[:, n % 3, :],
                                            ALU.mult).then_inc(hid, 1)
                elif step == "HL":
                    n = FC * g + u
                    dve.wait_ge(hid_hi, n + 1)
                    nc.vector.tensor_tensor(h_hl[:, n % 3, 1, :], hidden[:, n % 2, :], h_hl[:, n % 3, 0, :].bitcast(F32),
                                            ALU.subtract).then_inc(hid_lo, 1)

        @block.tensor
        def _(pe):
            def misc_free(step):
                if step in chain(1) and step != ("OTR", 1, 0):
                    pe.wait_ge(m_read, MISC[step] - 1)
                elif MISC[step] >= 1:
                    pe.wait_ge(m_read, MISC[step])

            pe.wait_ge(warm_set, 1)
            for _ in range(WARM):
                nc.tensor.matmul(s1_bank[0][:, :], warm[:, 0:P], warm[:, :], start=True, stop=True)

            for step, g, u in PLAN:
                misc = misc_bank((step, g, u)) if (step, g, u) in MISC else None
                if step in ("PROJ", "V"):
                    if g == 0 and (step == "PROJ" and u < 2 or step == "V" and u == 0):
                        pe.wait_ge(ld_w[1 - u % 2 if step == "PROJ" else 2], 16)
                    if step == "PROJ" and g == 1 and u == 0:
                        pe.wait_ge(ld_xT[KC], 16)
                    if (step, g, u) in EARLY:
                        n = EARLY[step, g, u]
                        dst = proj_bank[n % 3]
                        before = [s for s, m in EARLY.items() if m == n - 3]
                        if before and before[0][0] == "PROJ":
                            pe.wait_ge(qk_lo, 4 * before[0][1] + before[0][2] + 1)
                        elif before:
                            pe.wait_ge(v_done, 2 * before[0][1] + before[0][2] + 1)
                    else:
                        dst = misc
                        misc_free((step, g, u))
                    if step == "PROJ":
                        c = u // 2
                        for k in range(KC):
                            if g == 0 and u == 0:
                                pe.wait_ge(ld_xT[k], 16)
                            last = nc.tensor.matmul(dst[:, :], wqkv[:, 1 - u % 2, k, c * P:c * P + P],
                                                    xT[:, k, g * S:g * S + S], start=(k == 0), stop=(k == KC - 1))
                    else:
                        for m in range(2):
                            t = g * NT + 2 * u + m
                            for k in range(KC):
                                last = nc.tensor.matmul(dst[:, m * D:m * D + D], xT[:, k, t * P:t * P + P],
                                                        wqkv[:, 2, k, :], start=(k == 0), stop=(k == KC - 1))
                    last.then_inc(proj if (step, g, u) in EARLY else m_full, 1)
                elif step == "S1":
                    t, heads = UNITS1[u]
                    w = P * (t + 1)
                    n = NU * g + u
                    if u == 0:
                        pe.wait_ge(filled[SLOT[g]], 96 * FILLS[g])
                    if n >= 3:
                        pe.wait_ge(s1_read, n - 2)
                    for m, h in enumerate(heads):
                        last = nc.tensor.matmul(s1_bank[n % 3][:, m * w:m * w + w],
                                                stack[SLOT[g]][0:MAXROW, 1, h, t * P:t * P + P],
                                                stack[SLOT[g]][0:MAXROW, 0, h, 0:w], start=True, stop=True)
                    last.then_inc(s1, 1)
                elif step == "NM":
                    pe.wait_ge(s1_read, NU * (g + 1))
                    misc_free((step, g, u))
                    if g == 0:
                        pe.wait_ge(consts, IDENT_MADE)
                    nc.tensor.transpose(misc[0:QH * NT, 0:P], mx[:, g % 2].rearrange("p h t -> p (h t)"),
                                        ident[:, :]).then_inc(m_full, 1)
                elif step == "S2":
                    j, heads = UNITS2[u]
                    w = S - P * j
                    n = NU * g + u
                    if n == 0:
                        pe.wait_ge(qk_lo, EARLY_QK)
                        pe.wait_ge(v_done, EARLY_V)
                    if g == 1 and u == 0:
                        pe.wait_ge(ones_in, 16 * (SLOTS - 1))
                    if u == 0:
                        pe.wait_ge(nm_in[0], 16 * (g + 1))
                        pe.wait_ge(nm_in[1], 16 * (g + 1))
                    if n >= 3:
                        pe.wait_ge(exp_done, n - 2)
                    for m, h in enumerate(heads):
                        last = nc.tensor.matmul(s2_bank[n % 3][:, m * w:m * w + w],
                                                stack[SLOT[g]][0:MAXROW + 2, 0, h, j * P:j * P + P],
                                                stack[SLOT[g]][0:MAXROW + 2, 1, h, j * P:S], start=True, stop=True)
                    last.then_inc(s2, 1)
                elif step == "PV":
                    j = u
                    pe.wait_ge(masked, NT * g + j + 1)
                    if g == 0 and j == 0:
                        pe.wait_ge(consts, CONSTS)
                    if g >= 1 and j == 0:
                        pe.wait_ge(ot_copied, g)
                    for h in range(QH):
                        last = nc.tensor.matmul(pv_bank[32 * h:32 * h + VW, j * P:S],
                                                vv[:, g // NQ * NT + j, g % NQ * QH + h, :],
                                                pt[:, g % 2, h, SEG[j]:SEG[j] + S - P * j],
                                                start=(j == 0), stop=(j == NT - 1))
                    last.then_inc(pv, 1)
                elif step == "OT":
                    misc_free((step, g, u))
                    pe.wait_ge(ot_copied, g + 1)
                    for t in range(NT):
                        last = nc.tensor.transpose(misc[:, t * P:t * P + P], ot[:, g % 2, t * P:t * P + P], ident[:, :])
                    last.then_inc(m_full, 1)
                elif step == "OTR":
                    misc_free((step, g, u))
                    pe.wait_ge(attn_done, NQ * (g + 1))
                    for t in range(NT):
                        last = nc.tensor.transpose(misc[:, t * P:t * P + P], attn[:, t, u * P:u * P + P], ident[:, :])
                    last.then_inc(m_full, 1)
                elif step == "Y":
                    misc_free((step, g, u))
                    pe.wait_ge(m_read, MISC["OTR", g, 1] + 1)
                    pe.wait_ge(ld_wp, 16)
                    for m in range(2):
                        t = 2 * u + m
                        for k in range(KC):
                            last = nc.tensor.matmul(misc[:, m * D:m * D + D], attnT[:, k, t * P:t * P + P], wp[:, k, :],
                                                    start=(k == 0), stop=(k == KC - 1))
                    last.then_inc(m_full, 1)
                elif step == "XT":
                    misc_free((step, g, u))
                    pe.wait_ge(ln_done, 2 * (g + 1))
                    for t in range(NT):
                        last = nc.tensor.transpose(misc[:, t * P:t * P + P], x[:, g * NT + t, u * P:u * P + P], ident[:, :])
                    last.then_inc(m_full, 1)
                elif step == "RL":
                    misc_free((step, g, u))
                    pe.wait_ge(x1T_done, KC * (g + 1))
                    pe.wait_ge(consts, CONSTS_ALL)
                    for k in range(KC):
                        for part in (1, 0):
                            last = nc.tensor.matmul(misc[0:2 * E, :], wr[:, k, :], x1T[:, part, g, k, :],
                                                    start=(k == 0 and part == 1), stop=(k == KC - 1 and part == 0))
                    last.then_inc(m_full, 1)
                elif step == "RT":
                    misc_free((step, g, u))
                    pe.wait_ge(m_read, MISC["RL", g, 0] + 1)
                    for t in range(NT):
                        last = nc.tensor.transpose(misc[:, t * 2 * E:t * 2 * E + 2 * E], lgT[:, t * P:t * P + P],
                                                   ident[0:2 * E, 0:2 * E])
                    last.then_inc(m_full, 1)
                elif step == "RC":
                    misc_free((step, g, u))
                    pe.wait_ge(coef_done, g + 1)
                    for t in range(NT):
                        last = nc.tensor.transpose(misc[0:2 * E, t * P:t * P + P], coefhl[:, t, :], ident[:, :])
                    last.then_inc(m_full, 1)
                elif step == "GU":
                    n = FC * g + u
                    if n == 0:
                        pe.wait_ge(gu_split, PIECES)
                        pe.wait_ge(s1_read, NU * G)
                    if u == 0:
                        pe.wait_ge(x1T_done, KC * (g + 1))
                    for dst, col, done in ((gate_bank(n), u * P, gate), (up_bank(n), EI + u * P, up)):
                        if done is gate and n >= 2:
                            pe.wait_ge(gated_done, n - 1)
                        if done is up and n >= 1:
                            pe.wait_ge(silu_done, n)
                        for k in range(KC):
                            for w, part in ((gu_lo, 0), (gu_hi, 1), (gu_hi, 0)):
                                last = nc.tensor.matmul(dst[:, :], w[:, k, col:col + P], x1T[:, part, g, k, :],
                                                        start=(k == 0 and w is gu_lo), stop=(k == KC - 1 and w is gu_hi and part == 0))
                        last.then_inc(done, 1)
                elif step == "CB":
                    n = FC * g + u
                    if n == 0:
                        pe.wait_ge(exp_done, NU * G)
                    if u == 0:
                        pe.wait_ge(coefT_done, g + 1)
                    if n >= 1:
                        pe.wait_ge(hid, n)
                    nc.tensor.matmul(coef_bank[:, :], spread_r[:, u * P:u * P + P], coefT[:, g, :],
                                     start=True, stop=True).then_inc(coefs, 1)
                elif step == "YR":
                    for t in range(NT):
                        for k in range(KC):
                            for part in (1, 0):
                                col = t % 2 * D + k * P
                                nc.tensor.matmul(y_bank[g][t // 2][:, col:col + P], x1T[:, part, g, k, t * P:t * P + P],
                                                 ident_r[:, :], start=False, stop=False, skip_group_check=True)
                elif step == "DN":
                    n = FC * g + u
                    pe.wait_ge(hid_hi, n + 1)
                    pe.wait_ge(hid_lo, n + 1)
                    if n == 0:
                        pe.wait_ge(wd_split, FC)
                        pe.wait_ge(exp_done, NU * G)
                    if n == FC:
                        pe.wait_ge(m_read, len(MISC))
                    for t in range(NT):
                        for part, w in ((1, 0), (0, 1), (0, 0)):
                            last = nc.tensor.matmul(y_bank[g][t // 2][:, t % 2 * D:t % 2 * D + D],
                                                    h_hl[:, n % 3, part, t * P:t * P + P], wd_hl[:, w, u, :],
                                                    start=(u == 0 and t % 2 == 0 and part == 1),
                                                    stop=(u == FC - 1 and part == 0 and w == 0), skip_group_check=True)
                        if t % 2:
                            last.then_inc(down, 1)


def kernel(L0_attn_x, L0_attn_Wq, L0_attn_Wk, L0_attn_Wv, L0_attn_Wp, L0_ffn_router_w, L0_ffn_gate_w, L0_ffn_up_w, L0_ffn_down_w):
    import numpy as np
    import concourse.bacc as bacc
    from concourse.bass_utils import run_bass_kernel_spmd

    def rows(a):
        return np.ascontiguousarray(a.reshape(-1, P, a.shape[1]).transpose(1, 0, 2))

    def by_group(w):
        return w.T.reshape(D, NQ, QH, HD).transpose(0, 1, 3, 2).reshape(D, D)

    x = np.asarray(L0_attn_x).reshape(B * S, D)
    wq, wk, wv, wp = (np.asarray(w) for w in (L0_attn_Wq, L0_attn_Wk, L0_attn_Wv, L0_attn_Wp))
    gate, up, down = (np.asarray(w) for w in (L0_ffn_gate_w, L0_ffn_up_w, L0_ffn_down_w))
    arrays = {
        "xT": rows(x.T), "x": rows(x),
        "wqkv": np.ascontiguousarray(np.stack([rows(by_group(wq)), rows(by_group(wk)), rows(wv.T)], axis=1)),
        "wp": rows(wp.T), "wr": rows(np.asarray(L0_ffn_router_w).T),
        "wgu": rows(np.concatenate([gate.reshape(EI, D).T, up.reshape(EI, D).T], axis=1)),
        "wd": rows(down.transpose(0, 2, 1).reshape(EI, D)),
    }
    nc = bacc.Bacc("TRN2", target_bir_lowering=False, num_devices=1)
    aps = [nc.dram_tensor(n + "_dram", a.shape, mybir.dt.from_np(a.dtype), kind="ExternalInput").ap() for n, a in arrays.items()]
    out = nc.dram_tensor("out_dram", [P, B * NT, D], F32, kind="ExternalOutput").ap()
    layer_kernel(nc, *aps, out)
    r = run_bass_kernel_spmd(nc, [{n + "_dram": a for n, a in arrays.items()}], core_ids=[0])
    return np.ascontiguousarray(r.results[0]["out_dram"].transpose(1, 0, 2)).reshape(B, S, D)
```
